# Optimizing a Trainium2 kernel written in Bass

```python
import numpy as np
import jax
import jax.numpy as jnp

def _softmax(x, axis=-1):
    return jax.nn.softmax(x, axis=axis)

def _gelu(x):
    return jax.nn.gelu(x, approximate=True)

def _silu(x):
    return jax.nn.silu(x)

def _sigmoid(x):
    return jax.nn.sigmoid(x)

def _layernorm(x, axis=-1, eps=1e-05):
    m = jnp.mean(x, axis=axis, keepdims=True)
    v = jnp.var(x, axis=axis, keepdims=True)
    return (x - m) / jnp.sqrt(v + eps)

def _scatter_add(tgt, idx, src, axis=0):
    return tgt.at[idx].add(src)

def _segment_sum(src, seg, n):
    return jax.ops.segment_sum(src, seg, n)
kernel_name = 'mk_gnn_preln_d4_gnn_r8_904aba'

def setup_inputs(seed: int=0):
    np.random.seed(seed)
    _w = jnp.asarray

    def _rec_inputs():
        import jax
        import jax.numpy as jnp
        _gk = jax.random.key(seed)
        x = -0.0003713 + 1 * jax.random.normal(jax.random.fold_in(_gk, 1), (6250, 128), jnp.float32)
        _s = jax.random.randint(jax.random.fold_in(_gk, 2), (50000,), 0, 6250, jnp.int32)
        _d = jax.random.randint(jax.random.fold_in(_gk, 3), (50000,), 0, 6250, jnp.int32)
        _loop = jnp.arange(6250, dtype=jnp.int32)
        src = jnp.concatenate([_s, _d, _loop])
        dst = jnp.concatenate([_d, _s, _loop])
        _o = jnp.argsort(dst, stable=True)
        src = src[_o]
        dst = dst[_o]
        edge_attr_16 = -0.000191324 + 0.999809 * jax.random.normal(jax.random.fold_in(_gk, 11), (106250, 16), jnp.float32)
        return (x, src, dst, edge_attr_16)
    x, src, dst, edge_attr_16 = _rec_inputs()

    def _L0_gnn_setup():
        import jax, jax.numpy as jnp
        import numpy as np
        N = 12500
        E = 100000
        D_IN = 128
        D_OUT = 128
        ALPHA = 0.5

        def _mean_aggr(x, gather_idx, scatter_idx, num_nodes):
            summed = jax.ops.segment_sum(x[gather_idx], scatter_idx, num_segments=num_nodes)
            cnt = jax.ops.segment_sum(jnp.ones(gather_idx.shape, x.dtype), scatter_idx, num_segments=num_nodes)
            return summed / jnp.maximum(cnt, 1.0)[:, None]
        key = jax.random.key(seed)
        ks = jax.random.split(key, 8)
        x = jax.random.normal(ks[0], (N, D_IN), dtype=jnp.float32)
        edge_index = jax.random.randint(ks[1], (2, E), 0, N, dtype=jnp.int64)
        s = 1.0 / np.sqrt(D_IN)
        W_self = jax.random.uniform(ks[2], (D_IN, D_OUT), jnp.float32, -s, s)
        b_self = jax.random.uniform(ks[3], (D_OUT,), jnp.float32, -s, s)
        W_s2d = jax.random.uniform(ks[4], (D_IN, D_OUT), jnp.float32, -s, s)
        b_s2d = jnp.zeros((D_OUT,), jnp.float32)
        W_d2s = jax.random.uniform(ks[5], (D_IN, D_OUT), jnp.float32, -s, s)
        b_d2s = jnp.zeros((D_OUT,), jnp.float32)
        return {'x': x, 'W_self': W_self, 'b_self': b_self, 'W_s2d': W_s2d, 'b_s2d': b_s2d, 'W_d2s': W_d2s, 'b_d2s': b_d2s, 'edge_index': edge_index}
    _L0_gnn_all = _L0_gnn_setup()
    _L0_gnn_in = {k: v for k, v in _L0_gnn_all.items() if k in ('W_self', 'b_self', 'W_s2d', 'b_s2d', 'W_d2s', 'b_d2s')}
    del _L0_gnn_all

    def _L1_gnn_setup():
        import jax, jax.numpy as jnp
        import numpy as np
        N_NODES = 12500
        N_EDGES = 75000
        D_IN = 128
        D_HID = 128
        D_OUT = 128

        def _gcn_conv(x, W, b, src, dst, deg_inv_sqrt, n_nodes):
            h = x @ W
            norm = (deg_inv_sqrt[src] * deg_inv_sqrt[dst])[:, None]
            msg = h[src] * norm
            out = jax.ops.segment_sum(msg, dst, num_segments=n_nodes)
            return out + b
        key = jax.random.key(seed)
        k = jax.random.split(key, 6)
        x = jax.random.normal(k[0], (N_NODES, D_IN), dtype=jnp.float32)
        edge_index = jax.random.randint(k[1], (2, N_EDGES), 0, N_NODES, dtype=jnp.int64)
        W1 = jax.random.normal(k[2], (D_IN, D_HID), dtype=jnp.float32) / np.sqrt(D_IN)
        b1 = jnp.zeros((D_HID,), dtype=jnp.float32)
        W2 = jax.random.normal(k[3], (D_HID, D_OUT), dtype=jnp.float32) / np.sqrt(D_HID)
        b2 = jnp.zeros((D_OUT,), dtype=jnp.float32)
        return {'x': x, 'edge_index': edge_index, 'W1': W1, 'b1': b1, 'W2': W2, 'b2': b2}
    _L1_gnn_all = _L1_gnn_setup()
    _L1_gnn_in = {k: v for k, v in _L1_gnn_all.items() if k in ('W1', 'b1', 'W2', 'b2')}
    del _L1_gnn_all

    def _L2_gnn_setup():
        import jax, jax.numpy as jnp
        import numpy as np
        K = 3
        key = jax.random.key(seed)
        k1, k2 = jax.random.split(key)
        N, E, D = (12500, 400000, 128)
        h_local = jax.random.normal(k1, (N, D), dtype=jnp.float32)
        edge_list = jax.random.randint(k2, (2, E), 0, N, dtype=jnp.int64)
        return {'h_local': h_local, 'edge_list': edge_list, 'num_nodes': N}
    _L2_gnn_all = _L2_gnn_setup()
    _L2_gnn_in = {k: v for k, v in _L2_gnn_all.items() if k in ()}
    del _L2_gnn_all

    def _L3_gnn_setup():
        import jax, jax.numpy as jnp
        import numpy as np
        N_NODES = 1250
        N_EDGES = 40000
        IN_CH = 128
        LAYER = 128
        EDGE_DIM = 16

        def _edge_conv(x, src, dst, edge_attr, W, b, denom):
            msg = jnp.concatenate([x[src], edge_attr], axis=1) @ W + b
            s = jax.ops.segment_sum(msg, dst, num_segments=x.shape[0])
            return s / denom[:, None]
        key = jax.random.key(seed)
        ks = jax.random.split(key, 12)

        def w(k, shp):
            fan_in = shp[0]
            return jax.random.normal(k, shp, dtype=jnp.float32) / jnp.sqrt(jnp.float32(fan_in))
        return {'x': jax.random.normal(ks[0], (N_NODES, IN_CH), dtype=jnp.float32), 'edge_attr': jax.random.normal(ks[1], (N_EDGES, EDGE_DIM), dtype=jnp.float32), 'edge_index': jax.random.randint(ks[2], (2, N_EDGES), 0, N_NODES, dtype=jnp.int32), 'W0': w(ks[3], (IN_CH + EDGE_DIM, LAYER)), 'b0': jnp.zeros((LAYER,), jnp.float32), 'W1': w(ks[4], (LAYER + EDGE_DIM, LAYER)), 'b1': jnp.zeros((LAYER,), jnp.float32), 'W2': w(ks[5], (2 * LAYER + EDGE_DIM, LAYER)), 'b2': jnp.zeros((LAYER,), jnp.float32), 'W3': w(ks[6], (3 * LAYER + EDGE_DIM, LAYER)), 'b3': jnp.zeros((LAYER,), jnp.float32)}
    _L3_gnn_all = _L3_gnn_setup()
    _L3_gnn_in = {k: v for k, v in _L3_gnn_all.items() if k in ('W0', 'b0', 'W1', 'b1', 'W2', 'b2', 'W3', 'b3')}
    del _L3_gnn_all
    return {'x': x, 'src': src, 'dst': dst, 'edge_attr_16': edge_attr_16, 'L0_gnn_W_self': _L0_gnn_in['W_self'], 'L0_gnn_b_self': _L0_gnn_in['b_self'], 'L0_gnn_W_s2d': _L0_gnn_in['W_s2d'], 'L0_gnn_b_s2d': _L0_gnn_in['b_s2d'], 'L0_gnn_W_d2s': _L0_gnn_in['W_d2s'], 'L0_gnn_b_d2s': _L0_gnn_in['b_d2s'], 'L1_gnn_W1': _L1_gnn_in['W1'], 'L1_gnn_b1': _L1_gnn_in['b1'], 'L1_gnn_W2': _L1_gnn_in['W2'], 'L1_gnn_b2': _L1_gnn_in['b2'], 'L3_gnn_W0': _L3_gnn_in['W0'], 'L3_gnn_b0': _L3_gnn_in['b0'], 'L3_gnn_W1': _L3_gnn_in['W1'], 'L3_gnn_b1': _L3_gnn_in['b1'], 'L3_gnn_W2': _L3_gnn_in['W2'], 'L3_gnn_b2': _L3_gnn_in['b2'], 'L3_gnn_W3': _L3_gnn_in['W3'], 'L3_gnn_b3': _L3_gnn_in['b3']}

def reference(x, src, dst, edge_attr_16, L0_gnn_W_self, L0_gnn_b_self, L0_gnn_W_s2d, L0_gnn_b_s2d, L0_gnn_W_d2s, L0_gnn_b_d2s, L1_gnn_W1, L1_gnn_b1, L1_gnn_W2, L1_gnn_b2, L3_gnn_W0, L3_gnn_b0, L3_gnn_W1, L3_gnn_b1, L3_gnn_W2, L3_gnn_b2, L3_gnn_W3, L3_gnn_b3):
    import jax
    import jax.numpy as jnp

    def _L0_gnn_ref(x, W_self, b_self, W_s2d, b_s2d, W_d2s, b_d2s, edge_index):
        import jax, jax.numpy as jnp
        import numpy as np
        N = 12500
        E = 100000
        D_IN = 128
        D_OUT = 128
        ALPHA = 0.5

        def _mean_aggr(x, gather_idx, scatter_idx, num_nodes):
            summed = jax.ops.segment_sum(x[gather_idx], scatter_idx, num_segments=num_nodes)
            cnt = jax.ops.segment_sum(jnp.ones(gather_idx.shape, x.dtype), scatter_idx, num_segments=num_nodes)
            return summed / jnp.maximum(cnt, 1.0)[:, None]
        src, dst = (edge_index[0], edge_index[1])
        n = x.shape[0]
        agg_in = _mean_aggr(x, src, dst, n)
        agg_out = _mean_aggr(x, dst, src, n)
        out = x @ W_self + b_self + (1.0 - ALPHA) * (agg_in @ W_s2d + b_s2d) + ALPHA * (agg_out @ W_d2s + b_d2s)
        return out

    def _L1_gnn_ref(x, edge_index, W1, b1, W2, b2):
        import jax, jax.numpy as jnp
        import numpy as np
        N_NODES = 12500
        N_EDGES = 75000
        D_IN = 128
        D_HID = 128
        D_OUT = 128

        def _gcn_conv(x, W, b, src, dst, deg_inv_sqrt, n_nodes):
            h = x @ W
            norm = (deg_inv_sqrt[src] * deg_inv_sqrt[dst])[:, None]
            msg = h[src] * norm
            out = jax.ops.segment_sum(msg, dst, num_segments=n_nodes)
            return out + b
        n = x.shape[0]
        loops = jnp.arange(n, dtype=edge_index.dtype)
        src = jnp.concatenate([edge_index[0], loops])
        dst = jnp.concatenate([edge_index[1], loops])
        deg = jax.ops.segment_sum(jnp.ones_like(dst, dtype=x.dtype), dst, num_segments=n)
        deg_inv_sqrt = jax.lax.rsqrt(deg)
        h = _gcn_conv(x, W1, b1, src, dst, deg_inv_sqrt, n)
        h = jax.nn.relu(h)
        out = _gcn_conv(h, W2, b2, src, dst, deg_inv_sqrt, n)
        return out

    def _L2_gnn_ref(h_local, edge_list, num_nodes):
        import jax, jax.numpy as jnp
        import numpy as np
        K = 3
        N = num_nodes
        loops = jnp.broadcast_to(jnp.arange(N, dtype=edge_list.dtype)[None, :], (2, N))
        ei = jnp.concatenate([edge_list, loops], axis=1)
        row, col = (ei[0], ei[1])
        deg = jax.ops.segment_sum(jnp.ones_like(row, dtype=h_local.dtype), row, num_segments=N)
        deg_inv_sqrt = jnp.where(deg > 0, jax.lax.rsqrt(jnp.maximum(deg, 1.0)), 0.0)
        w = deg_inv_sqrt[row] * deg_inv_sqrt[col]

        def spmm(H):
            return jax.ops.segment_sum(w[:, None] * H[col], row, num_segments=N)
        H = h_local
        for _ in range(K):
            H = spmm(H)
        return H

    def _L3_gnn_ref(x, edge_attr, edge_index, W0, b0, W1, b1, W2, b2, W3, b3):
        import jax, jax.numpy as jnp
        import numpy as np
        N_NODES = 1250
        N_EDGES = 40000
        IN_CH = 128
        LAYER = 128
        EDGE_DIM = 16

        def _edge_conv(x, src, dst, edge_attr, W, b, denom):
            msg = jnp.concatenate([x[src], edge_attr], axis=1) @ W + b
            s = jax.ops.segment_sum(msg, dst, num_segments=x.shape[0])
            return s / denom[:, None]
        src, dst = (edge_index[0], edge_index[1])
        counts = jax.ops.segment_sum(jnp.ones((src.shape[0],), x.dtype), dst, num_segments=x.shape[0])
        denom = jnp.maximum(counts, 1.0)
        h = _edge_conv(x, src, dst, edge_attr, W0, b0, denom)
        outputs = [h]
        for W, b in ((W1, b1), (W2, b2), (W3, b3)):
            cat = jnp.concatenate(outputs, axis=1)
            z = _edge_conv(cat, src, dst, edge_attr, W, b, denom)
            outputs.append(z)
        return outputs[-1]
    edge_index = jnp.stack([src, dst])
    h = jnp.maximum(_layernorm(x, axis=-1), 0.0)
    x = x + _L0_gnn_ref(h, L0_gnn_W_self, L0_gnn_b_self, L0_gnn_W_s2d, L0_gnn_b_s2d, L0_gnn_W_d2s, L0_gnn_b_d2s, edge_index)
    h = jnp.maximum(_layernorm(x, axis=-1), 0.0)
    x = x + _L1_gnn_ref(h, edge_index, L1_gnn_W1, L1_gnn_b1, L1_gnn_W2, L1_gnn_b2)
    h = jnp.maximum(_layernorm(x, axis=-1), 0.0)
    x = x + _L2_gnn_ref(h, edge_index, 6250)
    h = jnp.maximum(_layernorm(x, axis=-1), 0.0)
    x = x + _L3_gnn_ref(h, edge_attr_16, edge_index, L3_gnn_W0, L3_gnn_b0, L3_gnn_W1, L3_gnn_b1, L3_gnn_W2, L3_gnn_b2, L3_gnn_W3, L3_gnn_b3)
    return x

_drawn_inputs = setup_inputs


def setup_inputs(seed=0):
    import zlib

    import numpy as np

    out = dict(_drawn_inputs(seed))
    spreads = {'L0_gnn_b_s2d': (0.0, 0.1),
     'L0_gnn_b_d2s': (0.0, 0.1),
     'L1_gnn_b1': (0.0, 0.1),
     'L1_gnn_b2': (0.0, 0.1),
     'L3_gnn_b0': (0.0, 0.1),
     'L3_gnn_b1': (0.0, 0.1),
     'L3_gnn_b2': (0.0, 0.1),
     'L3_gnn_b3': (0.0, 0.1)}
    factors = {}
    for name, (base, spread) in spreads.items():
        noise = np.random.default_rng([zlib.crc32(name.encode()), seed]).standard_normal(out[name].shape)
        drawn = base * np.exp(spread * noise) if base else spread * noise
        out[name] = jnp.asarray(drawn.astype(out[name].dtype))
    for name, factor in factors.items():
        out[name] = (out[name] * factor).astype(out[name].dtype)
    return out
```

```python
from contextlib import ExitStack

import numpy as np
import concourse.bass as bass
from concourse import mybir

N = 6250
E = 106250
D = 128
EDGE_DIM = 16
EC = EDGE_DIM + 1
EPS = 1e-5

P = 128
B = -(-N // P)
NP = B * P
LAST = N - (B - 1) * P
T = 832
FULL = E // T
REST = E - FULL * T
U = 4
K = 7
PAD = NP
ROWS = (B + 1) * P * B
SPARE = (NP + 1) * B + 1
EXACT = 256

F32 = mybir.dt.float32
BF16 = mybir.dt.bfloat16
I32 = mybir.dt.int32
U32 = mybir.dt.uint32
ALU = mybir.AluOpType
ACT = mybir.ActivationFunctionType
AX = mybir.AxisListType.X

STEPS = [
    dict(into="dst", loop=False, w=("s2d",), post="add_scaled", xin=0, xout=None),
    dict(into="src", loop=False, w=("d2s",), post="layer0_end", xin=0, xout=1),
    dict(into="dst", loop=True, w=("g1",), post="gcn_hidden", xin=1, xout=0),
    dict(into="dst", loop=True, w=("g2",), post="layer1_end", xin=0, xout=1),
    dict(into="src", loop=True, w=("ident",), post="hop", xin=1, xout=0),
    dict(into="src", loop=True, w=("ident",), post="hop", xin=0, xout=1),
    dict(into="src", loop=True, w=("ident",), post="layer2_end", xin=1, xout=0),
    dict(into="dst", loop=False, w=("e0",), edge="e0", post="edge0", xin=0, xout=1),
    dict(into="dst", loop=False, w=("e1", "e2a", "e3a"), edge="e1", post="edge1", xin=1, xout=0),
    dict(into="dst", loop=False, w=("e2b", "e3b"), edge="e2", post="edge2", xin=0, xout=1),
    dict(into="dst", loop=False, w=("e3c",), edge="e3", post="edge3", xin=1, xout=None),
]
NORM_LINKS = 5
POST_LINKS = dict(add_scaled=1, layer0_end=2 + NORM_LINKS, gcn_hidden=2, layer1_end=3 + NORM_LINKS, hop=1,
                  layer2_end=2 + NORM_LINKS, edge0=1, edge1=3, edge2=3, edge3=1)


NORMED_BEFORE = {"layer0_end": B, "layer1_end": 2 * B, "layer2_end": 3 * B}


def table_links(wide):
    return 1 if wide else 5


def post_links(step, wide):
    return POST_LINKS[step["post"]] + (table_links(wide) if step["xout"] is not None else 0)


def plan(wide):
    widths = [1] * K if wide else [2, 2, 2, 1]
    passes, posts, done, generation = [], 0, None, 0
    for s, step in enumerate(STEPS):
        b0 = 0
        for q, n in enumerate(widths):
            passes.append(dict(step=step, q=q, b0=b0, n=n, done=done, generation=generation))
            if done is not None:
                posts += K * done[2]
            done = (step, b0, n, posts)
            b0 += K * n
        if step["xout"] is not None:
            generation += 1
    return passes, done


def cuts(width):
    return [(c, min(512, width - c)) for c in range(0, width, 512)]


class Names:
    pass


def build_gnn(nc, a):
    ctx = ExitStack()
    with ctx:
        def sb(name, shape, dt=F32):
            return ctx.enter_context(nc.sbuf_tensor(name, shape, dt))

        def sem(name):
            return ctx.enter_context(nc.semaphore(name))

        m = Names()
        m.wide_of, m.narrow_of = {}, {}
        for into in ("dst", "src"):
            w = nc.dram_tensor(f"counts_into_{into}", (ROWS, P), F32, kind="Internal").ap()
            m.wide_of[into] = w
            m.narrow_of[into] = w.bitcast(BF16).rearrange("r (h c) -> (r h) c", h=2)[0:ROWS, :]
        m.edge_sums_dram = nc.dram_tensor("edge_sums_t", (EC, NP), F32, kind="Internal").ap()

        m.x = sb("x", [P, B, D])
        table0 = sb("table0", [P, B * 3 * D // 2])
        arena = sb("arena", [P, B * 3 * D // 2 + B * D + K * 2 * K * P // 2 + 2 * K * P])
        cut = [0]

        def part(n):
            cut[0] += n
            return arena[:, cut[0] - n:cut[0]]

        table1 = part(B * 3 * D // 2)
        m.carry = part(B * D).rearrange("p (b d) -> p b d", b=B)
        ring = part(K * 2 * K * P // 2)
        m.sums_t = part(2 * K * P)
        tables = [table0[:, :], table1]
        m.narrow_table = [t.bitcast(BF16).rearrange("p (b s d) -> p b s d", b=B, s=3) for t in tables]
        m.wide_table = [t[:, 0:B * D].rearrange("p (b d) -> p b d", b=B) for t in tables]
        m.staged = table0[:, B * D:B * D + K * D].rearrange("p (j d) -> p j d", j=K)
        m.ring_narrow = ring.bitcast(BF16).rearrange("p (j n) -> p j n", j=K)
        m.ring_wide = ring.rearrange("p (j n) -> p j n", j=K)
        m.edge_sums_t = table1[0:EC, 0:NP]
        cut[0] = 0
        m.attr = part(T * EDGE_DIM).rearrange("p (t c) -> p t c", c=EDGE_DIM)
        m.key = part(2 * T).rearrange("p (t w) -> p t w", w=2)
        m.lo = part(2 * T).rearrange("p (t w) -> p t w", w=2)
        m.hi = part(2 * T).rearrange("p (t w) -> p t w", w=2)
        raw = part(2 * T)
        m.raw = raw.bitcast(I32).rearrange("p (w t) -> p w t", w=2)
        m.zeros = part(NP // 4)
        m.key_cols = part(2 * U).rearrange("p (j w) -> p j w", w=2)
        m.lo_cols = part(2 * U).rearrange("p (j w) -> p j w", w=2)
        m.hi_cols = part(2 * U).rearrange("p (j w) -> p j w", w=2)
        m.attr_cols = part(U * EDGE_DIM).rearrange("p (j c) -> p j c", c=EDGE_DIM)
        m.rank = part(2 * U).rearrange("p (j w) -> p j w", w=2)
        m.late = part(2 * U).rearrange("p (j w) -> p j w", w=2)
        m.values_wide = part(2 * U * P).rearrange("p (j w c) -> p j w c", j=U, w=2)
        m.values = m.values_wide.rearrange("p j w c -> p (j w c)")[:, 0:U * P].bitcast(BF16).rearrange(
            "p (j w c) -> p j w c", j=U, w=2)
        m.index = sb("index", [P, 2 * U], U32)
        m.diag = sb("diag", [P, 2, 2, P])
        m.same = sb("same", [P, 2, 2, P], BF16)
        m.cell = sb("cell", [P, 2, 2, P], BF16)
        m.node_lo = sb("node_lo", [P, 2, P])
        m.weighted = sb("weighted", [P, 2, B, EC])
        m.node_hi = sb("node_hi", [P, 2, B], BF16)
        m.scratch = sb("scratch", [P, 2, P], BF16)

        m.ident = sb("ident", [P, P])
        m.ident_bf = sb("ident_bf", [P, P], BF16)
        m.before = sb("before", [P, P], BF16)
        m.ones = sb("ones", [P, P])
        m.iota = sb("iota", [P, P])
        m.iota_i = sb("iota_i", [P, P], I32)
        m.spare_i = sb("spare_i", [P, 1], I32)
        m.spare = sb("spare", [P, 1])
        m.zero_row = sb("zero_row", [P, 512], BF16)

        m.w_self = sb("w_self", [P, D])
        m.w = sb("w", [P, 11, D])
        names = ("s2d", "d2s", "g1", "g2", "e0", "e1", "e2a", "e3a", "e2b", "e3b", "e3c")
        m.w_at = {name: n for n, name in enumerate(names)}
        m.w_edge = sb("w_edge", [EC, 4, D])
        m.bias0 = sb("bias0", [1, 3, D])
        m.bias0_sum = sb("bias0_sum", [1, D])
        m.bias1 = sb("bias1", [P, 2, D])

        m.edge_sums = m.weighted[:, 0]
        m.n_src = sb("n_src", [P, B])
        m.scale = {k: sb(k, [P, B]) for k in ("inv_dst", "inv_src", "half_inv_dst", "half_inv_src",
                                              "dis_dst", "dis_src", "dis2_src")}
        m.most = sb("most", [P, 3])
        m.flag = sb("flag", [1, 4], I32)

        m.sums_slot = sb("sums_slot", [P, P])
        m.edge_slot = sb("edge_slot", [EC, P])
        m.edge_block = sb("edge_block", [P, EC])
        m.xn = sb("xn", [P, D])
        m.stats = sb("stats", [P, 6])
        m.meanvar = sb("meanvar", [P, 2])
        m.std = sb("std", [P, 1])
        m.rstd = sb("rstd", [P, 1])
        m.eps = sb("eps", [P, 1])
        m.nil = sb("nil", [P, 1])
        m.root = {end: sb(f"root_{end}", [P, B]) for end in ("dst", "src")}
        m.v = sb("v", [P, D])
        m.r = sb("r", [P, D])
        m.vt = sb("vt", [P, D])

        psum = ctx.enter_context(nc.psum_tensor("psum", [P, 8, 512], F32))
        m.acc = psum[:, 0:4, :].rearrange("p b n -> p (b n)")
        m.product = psum[:, 4, :]
        m.hist_dst = [psum[:, 0, 0:(B - B // 2) * EC], psum[:, 1, 0:(B // 2) * EC]]
        m.hist_banks = [psum[:, 0, :], psum[:, 1, :]]
        m.hist_src = psum[:, 1, 512 - B:512]
        pair = psum.rearrange("p b (h w c) -> p b h w c", h=2, w=2)[:, :, 0]
        m.joined = [pair[:, 2 + j] for j in range(2)]
        m.key_row = [pair[:, 4 + j] for j in range(U)]
        m.edge_row = psum[:, 5, :]

        s = Names()
        s.edges_in = sem("edges_in")
        s.cols_own = sem("cols_own")
        s.hist_own = sem("hist_own")
        s.rank_own = sem("rank_own")
        s.cell = sem("cell")
        s.most = sem("most")
        s.most_row = sem("most_row")
        s.zeroed = sem("zeroed")
        s.landed = sem("landed")
        s.var = sem("var")
        s.std = sem("std")
        s.degree = sem("degree")
        s.root = sem("root")
        s.loops_used = sem("loops_used")
        s.attr_in = sem("attr_in")
        s.x_in = sem("x_in")
        s.weights_in = sem("weights_in")
        s.consts = sem("consts")
        s.pads = sem("pads")
        s.zeros_set = sem("zeros_set")
        s.cols = sem("cols")
        s.diag = sem("diag")
        s.key_row = sem("key_row")
        s.same = sem("same")
        s.indexed = sem("indexed")
        s.joined = sem("joined")
        s.valued = sem("valued")
        s.hist_in = sem("hist_in")
        s.hist = sem("hist")
        s.flag_ready = sem("flag_ready")
        s.chain = sem("chain")
        s.pre_v = sem("pre_v")
        s.pre_t = sem("pre_t")
        s.pre_vt = sem("pre_vt")
        s.pre_done = sem("pre_done")
        s.edge_blk = sem("edge_blk")
        s.edge_t = sem("edge_t")
        s.edge_out = sem("edge_out")
        s.edge_stored = sem("edge_stored")
        s.into_dst = sem("into_dst")
        s.into_src = sem("into_src")
        s.wide_dst = sem("wide_dst")
        s.wide_src = sem("wide_src")
        s.rows_used = sem("rows_used")
        s.table_ready = sem("table_ready")
        s.evacuated = sem("evacuated")
        s.slot_ready = sem("slot_ready")
        s.edge_ready = sem("edge_ready")
        s.product_ready = sem("product_ready")
        s.product_read = sem("product_read")
        s.staged = sem("staged")
        s.final = sem("final")
        s.out_stored = sem("out_stored")
        s.ticks_pe = sem("ticks_pe")
        s.ticks_act = sem("ticks_act")
        s.ticks_dve = sem("ticks_dve")
        s.ticks_pool = sem("ticks_pool")
        s.rows_in = [sem(f"rows_in_{j}") for j in range(K)]
        s.spare_narrow, s.spare_wide = 2 * 16, 4 * 16

        block = ctx.enter_context(nc.Block())
        sync_program(nc, block, a, m, s)
        pool_program(nc, block, a, m, s)
        scalar_program(nc, block, a, m, s)
        vector_program(nc, block, a, m, s)
        tensor_program(nc, block, a, m, s)


def hold(eng, sem, value, ticks):
    eng.wait_ge(sem, value)
    eng.sem_inc(ticks, 1)


def rows_of(m, into, wide):
    flat = (m.wide_of if wide else m.narrow_of)[into]
    return flat.rearrange("(n b) c -> n (b c)", b=B)


def sync_program(nc, block, a, m, s):
    @block.sync
    def _(sp):
        sp.wait_ge(s.pads, 1)
        for w, ends in ((0, a.dst), (1, a.src)):
            sp.dma_start(m.raw[0:FULL, w, :], ends[0:FULL * T].rearrange("(p t) -> p t", t=T)).then_inc(s.edges_in, 16)
            sp.dma_start(m.raw[FULL:FULL + 1, w, 0:REST],
                         ends[FULL * T:E].rearrange("(p t) -> p t", p=1)).then_inc(s.edges_in, 16)
        sp.wait_ge(s.pads, 2)
        for b in range(0, B - 1, 16):
            sp.dma_start(m.x[:, b:b + 16, :], a.x[b * P:(b + 16) * P, :].rearrange("(b p) d -> p b d", p=P)).then_inc(
                s.x_in, 16)
        sp.dma_start(m.x[0:LAST, B - 1, :], a.x[(B - 1) * P:N, :]).then_inc(s.x_in, 16)
        for w in ("s2d", "d2s", "g1", "g2", "e0", "e1", "e2a", "e3a", "e2b", "e3b", "e3c"):
            sp.dma_start(m.w[:, m.w_at[w], :], a.w[w]).then_inc(s.weights_in, 16)
        sp.dma_start(m.w_self[:, :], a.w_self).then_inc(s.weights_in, 16)
        for n in range(4):
            sp.dma_start(m.w_edge[0:EDGE_DIM, n, :], a.w_edge[n]).then_inc(s.weights_in, 16)
            sp.dma_start(m.w_edge[EDGE_DIM:EC, n, :], a.b_edge[n].rearrange("(o d) -> o d", o=1)).then_inc(
                s.weights_in, 16)
        for n in range(3):
            sp.dma_start(m.bias0[0:1, n, :], a.bias0[n].rearrange("(o d) -> o d", o=1)).then_inc(s.weights_in, 16)
        for n in range(2):
            sp.dma_start(m.bias1[:, n, :], a.bias1[n].rearrange("(o d) -> o d", o=1).broadcast_to([P, D])).then_inc(
                s.weights_in, 16)
        sp.wait_ge(s.pads, 3)
        whole = T * EDGE_DIM
        attr = m.attr.rearrange("p t c -> p (t c)")
        source = a.edge_attr.rearrange("e c -> (e c)")
        for p0, p1 in ((0, 112), (112, FULL)):
            sp.dma_start(attr[p0:p1, :], source[p0 * whole:p1 * whole].rearrange("(p t) -> p t", t=whole)).then_inc(
                s.attr_in, 16)
        sp.dma_start(attr[FULL:FULL + 1, 0:REST * EDGE_DIM],
                     source[FULL * whole:].rearrange("(p t) -> p t", p=1)).then_inc(s.attr_in, 16)
        sp.wait_ge(s.zeros_set, 1)
        fill_zeros(sp, m, s, False)
        sp.wait_ge(s.edge_out, B)
        sp.dma_start(m.edge_sums_dram, m.edge_sums_t[:, :]).then_inc(s.edge_stored, 16)

        sp.wait_ge(s.flag_ready, 1)
        wide = sp.value_load(m.flag[0:1, 0:1])
        with sp.If(wide == 1):
            sp.wait_ge(s.into_dst, s.spare_narrow + 16 * T)
            sp.wait_ge(s.into_src, s.spare_narrow + 16 * T)
            sp.wait_ge(s.zeros_set, 2)
            fill_zeros(sp, m, s, True)
            stream_rows(sp, a, m, s, True)
        with sp.Else():
            stream_rows(sp, a, m, s, False)
        sp.wait_ge(s.out_stored, 2 * 16)


def fill_zeros(sp, m, s, wide):
    zeros = m.zeros if wide else m.zeros.bitcast(BF16)
    n = zeros.shape[1]
    for into in ("dst", "src"):
        rows = rows_of(m, into, wide)
        with sp.Fori(0, B) as b:
            for c in range(0, NP, n):
                sp.dma_start(rows[bass.ds(b * P, P), c:c + n], zeros).then_inc(s.zeroed, 16)


def stream_rows(sp, a, m, s, wide):
    passes, _ = plan(wide)
    ring = m.ring_wide if wide else m.ring_narrow
    start = (s.spare_wide if wide else s.spare_narrow) + 16 * T
    sp.wait_ge(s.wide_dst if wide else s.into_dst, start)
    sp.wait_ge(s.wide_src if wide else s.into_src, start)
    sp.wait_ge(s.edge_stored, 16)
    for g, ps in enumerate(passes):
        rows = rows_of(m, ps["step"]["into"], wide)
        width = ps["n"] * K * P
        with sp.Fori(0, K) as i:
            for j in range(K):
                sp.wait_ge(s.rows_used, i * K + (g * B + j + 1))
                sp.dma_start(ring[:, j, 0:width],
                             rows[bass.ds(i * (K * P) + j * P, P), ps["b0"] * P:ps["b0"] * P + width]).then_inc(
                                 s.rows_in[j], 16)
    sp.wait_ge(s.final, B)
    sp.dma_start(a.out[0:(B - 1) * P, :].rearrange("(b p) d -> p b d", p=P), m.x[:, 0:B - 1, :]).then_inc(
        s.out_stored, 16)
    sp.dma_start(a.out[(B - 1) * P:N, :], m.x[0:LAST, B - 1, :]).then_inc(s.out_stored, 16)


def pool_program(nc, block, a, m, s):
    @block.gpsimd
    def _(pool):
        pool.memset(m.raw, PAD).then_inc(s.pads, 1)
        pool.memset(m.x[:, B - 1, :], 0.0).then_inc(s.pads, 1)
        pool.memset(m.attr[:, REST:T, :], 0.0).then_inc(s.pads, 1)
        pool.iota(m.iota_i[:, :], pattern=[[1, P]], base=0, channel_multiplier=0).then_inc(s.consts, 1)
        pool.iota(m.spare_i[:, :], pattern=[[0, 1]], base=SPARE, channel_multiplier=1).then_inc(s.consts, 1)
        pool.memset(m.ones[:, :], 1.0).then_inc(s.consts, 1)
        pool.memset(m.zero_row[:, :], 0.0).then_inc(s.consts, 1)
        pool.memset(m.eps[:, :], EPS).then_inc(s.consts, 1)
        pool.memset(m.nil[:, :], 0.0).then_inc(s.consts, 1)
        pool.wait_ge(s.consts, 6)
        pool.affine_select(out=m.ident[:, :], in_=m.ones[:, :], compare_op=ALU.is_equal, fill=0.0,
                           base=0, pattern=[[-1, P]], channel_multiplier=1).then_inc(s.consts, 1)
        pool.affine_select(out=m.before[:, :], in_=m.ones[:, :], compare_op=ALU.is_gt, fill=0.0,
                           base=0, pattern=[[-1, P]], channel_multiplier=1).then_inc(s.consts, 1)
        pool.wait_ge(s.consts, 8)
        pool.tensor_copy(m.ident_bf[:, :], m.ident[:, :]).then_inc(s.consts, 1)
        pool.sem_inc(s.landed, U)
        add_edges(pool, m, s, False)

        pool.wait_ge(s.flag_ready, 1)
        wide = pool.value_load(m.flag[0:1, 0:1])
        with pool.If(wide == 1):
            add_edges(pool, m, s, True)
            feed_blocks(pool, m, s, True)
        with pool.Else():
            feed_blocks(pool, m, s, False)


def add_edges(pool, m, s, wide):
    values = m.values_wide if wide else m.values
    done = (s.wide_dst, s.wide_src) if wide else (s.into_dst, s.into_src)
    flat = m.wide_of if wide else m.narrow_of
    before = T if wide else 0
    zeros = m.zeros if wide else m.zeros.bitcast(BF16)
    n = zeros.shape[1]
    spare = 16 * (NP // n)
    pool.wait_ge(s.zeros_set, 2 if wide else 1)
    if wide:
        pool.wait_ge(s.into_dst, s.spare_narrow + 16 * T)
        pool.wait_ge(s.into_src, s.spare_narrow + 16 * T)
    for w, into in enumerate(("dst", "src")):
        for c in range(0, NP, n):
            pool.dma_start(rows_of(m, into, wide)[B * P:(B + 1) * P, c:c + n], zeros).then_inc(done[w], 16)
    pool.wait_ge(s.zeroed, 2 * B * (s.spare_narrow + (s.spare_wide if wide else 0)))
    with pool.Fori(0, T // U) as g:
        for j in range(U):
            hold(pool, s.valued, g * U + (before + j + 3), s.ticks_pool)
            hold(pool, s.indexed, g * U + (before + j + 1), s.ticks_pool)
            for w, into in enumerate(("dst", "src")):
                hold(pool, done[w], g * (16 * U) + (spare + 16 * j), s.ticks_pool)
                if into == "src":
                    pool.sem_inc(s.landed, 1)
                pool.indirect_dma_start(
                    out=flat[into], out_offset=bass.IndirectOffsetOnAxis(ap=m.index[:, 2 * j + w:2 * j + w + 1], axis=0),
                    in_=values[:, j, w, :], in_offset=None, compute_op=ALU.add).then_inc(done[w], 16)


def feed_blocks(pool, m, s, wide):
    passes, last = plan(wide)
    loops = 1

    def feed(done, i, p):
        _, b0, n, posts = done
        hold(pool, s.product_ready, i * n + (posts + p + 1), s.ticks_pool)
        pool.dma_start(m.edge_slot[:, :], m.edge_sums_dram[:, bass.ds(i * (n * P) + (b0 + p) * P, P)]).then_inc(
            s.edge_ready, 16)

    def stage(ps, block_at, j, used):
        hold(pool, s.table_ready, block_at + (ps["generation"] * B + 1), s.ticks_pool)
        hold(pool, s.rows_used, used, s.ticks_pool)
        pool.wait_ge(s.loops_used, loops)
        pool.tensor_copy(m.staged[:, j, :], m.wide_table[ps["step"]["xin"]][:, bass.ds(block_at, 1), :].rearrange(
            "p o d -> p (o d)")).then_inc(s.staged, 1)

    pool.wait_ge(s.edge_stored, 16)
    for g, ps in enumerate(passes):
        done = ps["done"]
        feeds = done is not None and "edge" in done[0]
        if wide and ps["step"]["loop"]:
            for j in range(K):
                stage(ps, ps["b0"] + j, j, g * B + j + 1)
            loops += K
        if not (feeds or wide):
            continue
        with pool.Fori(0, K) as i:
            for j in range(K):
                if wide:
                    stage(ps, i * K + j, j, i * K + (g * B + j + 1))
                if feeds and j in post_slots(done[2]):
                    feed(done, i, post_slots(done[2]).index(j))
    with pool.Fori(0, K) as i:
        for p in range(last[2]):
            feed(last, i, p)


def post_slots(n):
    return [3] if n == 1 else [2, 5]


def scalar_program(nc, block, a, m, s):
    @block.scalar
    def _(act):
        act.wait_ge(s.consts, 9)
        act.sem_inc(s.valued, 2)
        with act.Fori(0, B) as b:
            deviation(nc, act, m, s, b)
            hold(act, s.pre_t, b + 1, s.ticks_act)
            nc.scalar.copy(m.vt[:, :], m.product[:, 0:P]).then_inc(s.pre_vt, 1)
        spread_keys(nc, act, m, s, False)
        act.wait_ge(s.degree, 2)
        for end in ("dst", "src"):
            nc.scalar.activation(m.root[end][:, :], m.scale[f"dis_{end}"][:, :], ACT.Sqrt, bias=m.nil[:, :]).then_inc(
                s.root, 1)
        with act.Fori(0, B) as b:
            hold(act, s.edge_t, b + 1, s.ticks_act)
            nc.scalar.copy(m.edge_sums_t[:, bass.ds(b * P, P)], m.edge_row[0:EC, 0:P]).then_inc(s.edge_out, 1)

        act.wait_ge(s.flag_ready, 1)
        wide = act.value_load(m.flag[0:1, 0:1])
        with act.If(wide == 1):
            act.wait_ge(s.into_dst, s.spare_narrow + 16 * T)
            act.wait_ge(s.into_src, s.spare_narrow + 16 * T)
            spread_keys(nc, act, m, s, True)
            hand_over_sums(nc, act, m, s, True)
        with act.Else():
            hand_over_sums(nc, act, m, s, False)


def deviation(nc, act, m, s, index):
    hold(act, s.var, index + 1, s.ticks_act)
    nc.scalar.activation(m.std[:, :], m.meanvar[:, 1:2], ACT.Sqrt, bias=m.eps[:, :]).then_inc(s.std, 1)


def spread_keys(nc, act, m, s, wide):
    values = m.values_wide if wide else m.values
    t0 = T if wide else 0
    with act.Fori(0, T // U) as g:
        hold(act, s.cols, g + (t0 // U + 1), s.ticks_act)
        for j in range(U):
            if j >= 2:
                hold(act, s.key_row, g * U + (t0 + j - 1), s.ticks_act)
            for w in range(2):
                last = nc.scalar.activation(m.diag[:, j % 2, w, :], m.ident[:, :], ACT.Copy,
                                            scale=m.key_cols[:, j, w:w + 1])
            last.then_inc(s.diag, 1)
        for j in range(U):
            hold(act, s.joined, g * U + (t0 + j + 3), s.ticks_act)
            hold(act, s.landed, g * U + (t0 + j + 2), s.ticks_act)
            nc.scalar.copy(values[:, j, :, :], m.joined[j % 2]).then_inc(s.valued, 1)


def hand_over_sums(nc, act, m, s, wide):
    passes, last = plan(wide)
    evacuated = 0
    for g, ps in enumerate(passes):
        width = ps["n"] * K * P
        act.wait_ge(s.rows_used, K + (g + 1) * B)
        for c, n in cuts(width):
            nc.scalar.copy(m.sums_t[:, c:c + n], m.acc[:, c:c + n]).then_inc(s.evacuated, 1)
            evacuated += 1
        done = passes[g + 1]["done"] if g + 1 < len(passes) else last
        step, b0, n, posts = done
        act.wait_ge(s.evacuated, evacuated)
        with act.Fori(0, K) as i:
            for p in range(n):
                hold(act, s.product_ready, i * n + (posts + p + 1), s.ticks_act)
                nc.scalar.copy(m.sums_slot[:, :], m.sums_t[:, bass.ds(i * (n * P) + p * P, P)]).then_inc(
                    s.slot_ready, 1)
                if step["post"] in NORMED_BEFORE:
                    deviation(nc, act, m, s, i * n + (b0 + p + NORMED_BEFORE[step["post"]]))


class Chain:

    def __init__(self, dve, sem):
        self.dve, self.sem, self.base, self.at, self.turn, self.each = dve, sem, 0, 0, None, 0

    def enter(self, turn, each):
        self.turn, self.each, self.at = turn, each, 0

    def leave(self, rounds):
        assert self.at == self.each, (self.at, self.each)
        self.base += rounds * self.each
        self.turn = None

    def link(self, instruction):
        instruction.then_inc(self.sem, 1)
        if self.turn is None:
            self.base += 1
            self.dve.wait_ge(self.sem, self.base)
        else:
            self.at += 1
            self.dve.wait_ge(self.sem, self.turn * self.each + (self.base + self.at))


def one(tensor, b):
    return tensor[:, bass.ds(b, 1), :].rearrange("p o d -> p (o d)")


def normalize(nc, dve, chain, m, s, index, scale=None):
    v = nc.vector
    chain.link(v.bn_stats(m.stats[:, :], m.xn[:, :]))
    dve.sem_inc(s.ticks_dve, 1)
    chain.link(v.bn_aggr(m.meanvar[:, :], m.stats[:, :]))
    dve.sem_inc(s.var, 1)
    hold(dve, s.std, index + 1, s.ticks_dve)
    chain.link(v.reciprocal(m.rstd[:, :], m.std[:, :]))
    chain.link(v.tensor_scalar(m.r[:, :], m.xn[:, :], m.meanvar[:, 0:1], m.rstd[:, :],
                               op0=ALU.subtract, op1=ALU.mult))
    if scale is None:
        chain.link(v.tensor_scalar(m.v[:, :], m.r[:, :], 0.0, None, op0=ALU.max))
    else:
        chain.link(v.tensor_scalar(m.v[:, :], m.r[:, :], 0.0, scale, op0=ALU.max, op1=ALU.mult))


def write_table(nc, dve, chain, m, s, table, b, wide):
    v = nc.vector
    if wide:
        chain.link(v.tensor_scalar(one(m.wide_table[table], b), m.v[:, :], 1.0, None, op0=ALU.mult))
    else:
        hi, mid, lo = (m.narrow_table[table][:, bass.ds(b, 1), n, :].rearrange("p o d -> p (o d)") for n in range(3))
        chain.link(v.tensor_scalar(hi, m.v[:, :], 1.0, None, op0=ALU.mult))
        chain.link(v.tensor_tensor(m.r[:, :], m.v[:, :], hi, op=ALU.subtract))
        chain.link(v.tensor_scalar(mid, m.r[:, :], 1.0, None, op0=ALU.mult))
        chain.link(v.tensor_tensor(m.xn[:, :], m.r[:, :], mid, op=ALU.subtract))
        chain.link(v.tensor_scalar(lo, m.xn[:, :], 1.0, None, op0=ALU.mult))
    dve.sem_inc(s.table_ready, 1)


def vector_program(nc, block, a, m, s):
    @block.vector
    def _(dve):
        v = nc.vector
        chain = Chain(dve, s.chain)
        dve.wait_ge(s.consts, 9)
        chain.link(v.tensor_copy(m.iota[:, :], m.iota_i[:, :]))
        chain.link(v.tensor_copy(m.spare[:, :], m.spare_i[:, :]))
        dve.wait_ge(s.pads, 3)
        v.memset(m.zeros, 0.0).then_inc(s.zeros_set, 1)

        dve.wait_ge(s.edges_in, 4 * 16)
        whole = m.key.rearrange("p t w -> p (t w)").bitcast(I32).rearrange("p (w t) -> p w t", w=2)
        chain.link(v.tensor_single_scalar(whole, m.raw, P - 1, op=ALU.bitwise_and))
        chain.link(v.tensor_copy(m.lo.rearrange("p t w -> p w t"), whole))
        chain.link(v.tensor_single_scalar(whole, m.raw, 7, op=ALU.logical_shift_right))
        chain.link(v.tensor_copy(m.hi.rearrange("p t w -> p w t"), whole))
        for w in range(2):
            chain.link(v.scalar_tensor_tensor(m.key[:, :, w], m.hi[:, :, 1 - w], float(P), m.lo[:, :, 1 - w],
                                              op0=ALU.mult, op1=ALU.add))
            chain.link(v.scalar_tensor_tensor(m.key[:, :, w], m.key[:, :, w], float(B), m.hi[:, :, w],
                                              op0=ALU.mult, op1=ALU.add))

        dve.wait_ge(s.x_in, 4 * 16)
        dve.wait_ge(s.weights_in, 25 * 16)
        chain.link(v.tensor_tensor(m.bias0_sum[:, :], m.bias0[:, 1, :], m.bias0[:, 2, :], op=ALU.add))
        chain.link(v.scalar_tensor_tensor(m.bias0_sum[:, :], m.bias0_sum[:, :], 0.5, m.bias0[:, 0, :],
                                          op0=ALU.mult, op1=ALU.add))
        with dve.Fori(0, B) as b:
            chain.enter(b, 1 + NORM_LINKS + table_links(False) + 1)
            chain.link(v.tensor_scalar(m.xn[:, :], one(m.x, b), 1.0, None, op0=ALU.mult))
            normalize(nc, dve, chain, m, s, b)
            dve.sem_inc(s.pre_v, 1)
            write_table(nc, dve, chain, m, s, 0, b, False)
            hold(dve, s.pre_done, b + 1, s.ticks_dve)
            chain.link(v.tensor_tensor(one(m.x, b), m.product[:, 0:D], one(m.x, b), op=ALU.add))
        chain.leave(B)

        dve.wait_ge(s.attr_in, 3 * 16)
        index_edges(nc, dve, chain, m, s, False)

        dve.wait_ge(s.hist, T + 2)
        half = B - B // 2
        chain.link(v.tensor_copy(m.edge_sums[:, 0:half, :].rearrange("p b c -> p (b c)"), m.hist_dst[0]))
        chain.link(v.tensor_copy(m.edge_sums[:, half:B, :].rearrange("p b c -> p (b c)"), m.hist_dst[1]))
        chain.link(v.tensor_copy(m.n_src[:, :], m.hist_src))
        n_dst = m.edge_sums[:, :, EDGE_DIM]
        for end, n in (("dst", n_dst), ("src", m.n_src[:, :])):
            inv, half_inv = m.scale[f"inv_{end}"][:, :], m.scale[f"half_inv_{end}"][:, :]
            chain.link(v.tensor_scalar(inv, n, 1.0, None, op0=ALU.max))
            chain.link(v.reciprocal(inv, inv))
            chain.link(v.tensor_scalar(half_inv, inv, 0.5, None, op0=ALU.mult))
            chain.link(v.tensor_scalar(m.scale[f"dis_{end}"][:, :], n, 1.0, None, op0=ALU.add))
            dve.sem_inc(s.degree, 1)
        dve.wait_ge(s.root, 2)
        for end in ("dst", "src"):
            chain.link(v.reciprocal(m.scale[f"dis_{end}"][:, :], m.root[end][:, :]))
        chain.link(v.tensor_tensor(m.scale["dis2_src"][:, :], m.scale["dis_src"][:, :], m.scale["dis_src"][:, :],
                                   op=ALU.mult))
        chain.link(v.tensor_reduce(out=m.most[:, 0:1], in_=n_dst, axis=AX, op=ALU.max))
        chain.link(v.tensor_reduce(out=m.most[:, 1:2], in_=m.n_src[:, :], axis=AX, op=ALU.max))
        v.tensor_tensor(m.most[:, 2:3], m.most[:, 0:1], m.most[:, 1:2], op=ALU.max).then_inc(s.most, 1)
        dve.wait_ge(s.most_row, 1)
        chain.link(v.tensor_reduce(out=m.rstd[0:1, 0:1], in_=m.product[0:1, 0:P], axis=AX, op=ALU.max))
        v.tensor_scalar(m.flag[0:1, 0:1], m.rstd[0:1, 0:1], float(EXACT), None, op0=ALU.is_gt).then_inc(
            s.flag_ready, 1)
        with dve.Fori(0, B) as b:
            v.tensor_scalar(m.edge_block[:, :], one(m.edge_sums, b), 1.0, None, op0=ALU.mult).then_inc(s.edge_blk, 1)
            hold(dve, s.edge_out, b + 1, s.ticks_dve)

        dve.wait_ge(s.flag_ready, 1)
        wide = dve.value_load(m.flag[0:1, 0:1])
        before = chain.base
        with dve.If(wide == 1):
            dve.wait_ge(s.edge_stored, 16)
            with dve.Fori(0, B) as b:
                chain.enter(b, 3)
                hi, mid, lo = (m.narrow_table[0][:, bass.ds(b, 1), n, :].rearrange("p o d -> p (o d)")
                               for n in range(3))
                chain.link(v.tensor_tensor(m.r[:, :], hi, mid, op=ALU.add))
                chain.link(v.tensor_tensor(m.v[:, :], m.r[:, :], lo, op=ALU.add))
                chain.link(v.tensor_scalar(one(m.wide_table[0], b), m.v[:, :], 1.0, None, op0=ALU.mult))
            chain.leave(B)
            v.memset(m.zeros, 0.0).then_inc(s.zeros_set, 1)
            dve.wait_ge(s.into_dst, s.spare_narrow + 16 * T)
            dve.wait_ge(s.into_src, s.spare_narrow + 16 * T)
            index_edges(nc, dve, chain, m, s, True)
            finish_blocks(nc, dve, chain, m, s, True)
        with dve.Else():
            chain.base = before
            finish_blocks(nc, dve, chain, m, s, False)


def index_edges(nc, dve, chain, m, s, wide):
    v = nc.vector
    t0 = T if wide else 0
    with dve.Fori(0, T // U) as g:
        chain.enter(g, 3 * U)
        if wide:
            hold(dve, s.key_row, g * U + t0, s.ticks_dve)
        v.tensor_scalar(m.hi_cols, m.hi[:, bass.ds(g * U, U), :], 1.0, None, op0=ALU.mult).then_inc(s.cols_own, 1)
        v.tensor_scalar(m.lo_cols, m.lo[:, bass.ds(g * U, U), :], 1.0, None, op0=ALU.mult).then_inc(s.cols_own, 1)
        v.tensor_scalar(m.attr_cols, m.attr[:, bass.ds(g * U, U), :], 1.0, None, op0=ALU.mult).then_inc(s.cols_own, 1)
        v.tensor_scalar(m.key_cols, m.key[:, bass.ds(g * U, U), :], 1.0, None, op0=ALU.mult).then_inc(s.cols, 1)
        hold(dve, s.cols, g + (t0 // U + 1), s.ticks_dve)
        hold(dve, s.cols_own, g * 3 + (3 * t0 // U + 3), s.ticks_dve)
        for j in range(U):
            t = g * U + (t0 + j)
            slot = j % 2
            hold(dve, s.joined, t + 1, s.ticks_dve)
            if not wide:
                hold(dve, s.hist, t + 1, s.ticks_dve)
                v.tensor_scalar(m.node_lo[:, slot, :], m.iota[:, :], m.lo_cols[:, j, 0:1], None,
                                op0=ALU.is_equal).then_inc(s.hist_own, 1)
                v.tensor_scalar(m.node_hi[:, slot, :], m.iota[:, 0:B], m.hi_cols[:, j, 1:2], None,
                                op0=ALU.is_equal).then_inc(s.hist_own, 1)
                v.tensor_scalar(m.weighted[:, slot, :, EDGE_DIM], m.iota[:, 0:B], m.hi_cols[:, j, 0:1], None,
                                op0=ALU.is_equal).then_inc(s.hist_own, 1)
            v.tensor_tensor(m.cell[:, slot, :, :], m.iota[:, :].unsqueeze(1).broadcast_to([P, 2, P]),
                            m.lo_cols[:, j, :].unsqueeze(2).broadcast_to([P, 2, P]),
                            op=ALU.is_equal).then_inc(s.cell, 1)
            hold(dve, s.key_row, t + 1, s.ticks_dve)
            v.tensor_tensor(m.same[:, slot, :, :], m.key_row[j],
                            m.key_cols[:, j, :].unsqueeze(2).broadcast_to([P, 2, P]),
                            op=ALU.is_equal).then_inc(s.same, 1)
            if not wide:
                hold(dve, s.hist_own, g * (3 * U) + (3 * j + 3), s.ticks_dve)
                v.tensor_tensor(m.weighted[:, slot, :, 0:EDGE_DIM],
                                m.attr_cols[:, j, :].unsqueeze(1).broadcast_to([P, B, EDGE_DIM]),
                                m.weighted[:, slot, :, EDGE_DIM:EC].broadcast_to([P, B, EDGE_DIM]),
                                op=ALU.mult).then_inc(s.hist_in, 1)
            hold(dve, s.same, t + 1, s.ticks_dve)
            for w in range(2):
                last = v.tensor_tensor_reduce(out=m.scratch[:, w, :], in0=m.same[:, slot, w, :], in1=m.before[:, :],
                                              scale=1.0, scalar=0.0, op0=ALU.mult, op1=ALU.add,
                                              accum_out=m.rank[:, j, w:w + 1])
                if w == 0:
                    last.then_inc(s.rank_own, 1)
            chain.link(last)
            hold(dve, s.rank_own, t + 1, s.ticks_dve)
            chain.link(v.tensor_scalar(m.late[:, j, :], m.rank[:, j, :], 0.5, m.spare[:, :], op0=ALU.is_gt,
                                       op1=ALU.mult))
            hold(dve, s.landed, t + 2, s.ticks_dve)
            chain.link(v.tensor_tensor(m.index[:, 2 * j:2 * j + 2], m.late[:, j, :], m.key_cols[:, j, :], op=ALU.max))
            dve.sem_inc(s.indexed, 1)
    chain.leave(T // U)


def finish_blocks(nc, dve, chain, m, s, wide):
    passes, last = plan(wide)
    v = nc.vector
    windows = [ps["done"] for ps in passes if ps["done"] is not None] + [last]
    for step, b0, n, posts in windows:
        normed = NORMED_BEFORE.get(step["post"], 0)
        each = post_links(step, wide)
        with dve.Fori(0, K) as i:
            chain.enter(i, each * n)
            for p in range(n):
                b = i * n + (b0 + p)
                hold(dve, s.product_ready, i * n + (posts + p + 2), s.ticks_dve)
                finish_block(nc, dve, chain, m, s, step, b, b + normed, wide)
        chain.leave(K)


def finish_block(nc, dve, chain, m, s, step, b, normed, wide):
    v = nc.vector
    post = step["post"]
    x = one(m.x, b)
    part = [m.product[:, D * n:D * (n + 1)] for n in range(3)]

    def by(name):
        return m.scale[name][:, bass.ds(b, 1)]

    def read():
        dve.sem_inc(s.product_read, 1)

    if post == "add_scaled":
        chain.link(v.scalar_tensor_tensor(x, part[0], by("half_inv_dst"), x, op0=ALU.mult, op1=ALU.add))
        read()
    elif post in ("layer0_end", "layer1_end", "layer2_end"):
        own, following = {"layer0_end": ("half_inv_src", "dis_dst"), "layer1_end": ("dis_dst", "dis_src"),
                          "layer2_end": ("dis_src", None)}[post]
        chain.link(v.scalar_tensor_tensor(m.xn[:, :], part[0], by(own), x, op0=ALU.mult, op1=ALU.add))
        read()
        if post == "layer1_end":
            chain.link(v.tensor_tensor(m.xn[:, :], m.xn[:, :], m.bias1[:, 1, :], op=ALU.add))
        chain.link(v.tensor_scalar(x, m.xn[:, :], 1.0, None, op0=ALU.mult))
        normalize(nc, dve, chain, m, s, normed, by(following) if following else None)
    elif post == "gcn_hidden":
        chain.link(v.scalar_tensor_tensor(m.r[:, :], part[0], by("dis_dst"), m.bias1[:, 0, :],
                                          op0=ALU.mult, op1=ALU.add))
        read()
        chain.link(v.tensor_scalar(m.v[:, :], m.r[:, :], 0.0, by("dis_dst"), op0=ALU.max, op1=ALU.mult))
    elif post == "hop":
        chain.link(v.tensor_scalar(m.v[:, :], part[0], by("dis2_src"), None, op0=ALU.mult))
        read()
    elif post == "edge0":
        chain.link(v.tensor_scalar(m.v[:, :], part[0], by("inv_dst"), None, op0=ALU.mult))
        read()
    elif post == "edge1":
        chain.link(v.tensor_scalar(m.v[:, :], part[0], by("inv_dst"), None, op0=ALU.mult))
        chain.link(v.tensor_scalar(one(m.carry, b), part[1], 1.0, None, op0=ALU.mult))
        chain.link(v.scalar_tensor_tensor(x, part[2], by("inv_dst"), x, op0=ALU.mult, op1=ALU.add))
        read()
    elif post == "edge2":
        chain.link(v.tensor_tensor(m.r[:, :], part[0], one(m.carry, b), op=ALU.add))
        chain.link(v.scalar_tensor_tensor(x, part[1], by("inv_dst"), x, op0=ALU.mult, op1=ALU.add))
        read()
        chain.link(v.tensor_scalar(m.v[:, :], m.r[:, :], by("inv_dst"), None, op0=ALU.mult))
    elif post == "edge3":
        chain.link(v.scalar_tensor_tensor(x, part[0], by("inv_dst"), x, op0=ALU.mult, op1=ALU.add))
        read()
        dve.sem_inc(s.final, 1)
    if step["xout"] is not None:
        write_table(nc, dve, chain, m, s, step["xout"], b, wide)


def tensor_program(nc, block, a, m, s):
    @block.tensor
    def _(pe):
        mm = nc.tensor.matmul
        pe.wait_ge(s.consts, 9)
        pe.wait_ge(s.weights_in, 25 * 16)
        with pe.Fori(0, B) as b:
            hold(pe, s.pre_v, b + 1, s.ticks_pe)
            mm(m.product[:, 0:P], m.v[:, :], m.ident[:, :], start=True, stop=True).then_inc(s.pre_t, 1)
            hold(pe, s.pre_vt, b + 1, s.ticks_pe)
            mm(m.product[:, 0:D], m.vt[:, :], m.w_self[:, :], start=True, stop=False)
            mm(m.product[:, 0:D], m.ones[0:1, :], m.bias0_sum[:, :], start=False, stop=True).then_inc(s.pre_done, 1)

        zero = m.zero_row[:, 0:P]
        for bank in m.hist_banks:
            mm(bank, zero, m.zero_row[:, :], start=True, stop=True, skip_group_check=True)
        pe.sem_inc(s.joined, 2)
        pe.sem_inc(s.hist, 2)
        join_edges(nc, pe, m, s, False)
        pe.wait_ge(s.most, 1)
        mm(m.product[0:1, 0:P], m.most[:, 2:3], m.ident[:, :], start=True, stop=True).then_inc(s.most_row, 1)
        with pe.Fori(0, B) as b:
            hold(pe, s.edge_blk, b + 1, s.ticks_pe)
            mm(m.edge_row[0:EC, 0:P], m.edge_block[:, :], m.ident[:, :], start=True, stop=True).then_inc(s.edge_t, 1)

        pe.sem_inc(s.rows_used, K)
        pe.sem_inc(s.product_ready, 1)
        pe.sem_inc(s.product_read, 1)
        pe.sem_inc(s.loops_used, 1)
        pe.wait_ge(s.flag_ready, 1)
        wide = pe.value_load(m.flag[0:1, 0:1])
        with pe.If(wide == 1):
            join_edges(nc, pe, m, s, True)
            multiply(nc, pe, m, s, True)
        with pe.Else():
            multiply(nc, pe, m, s, False)


def join_edges(nc, pe, m, s, wide):
    mm = nc.tensor.matmul
    t0 = T if wide else 0
    with pe.Fori(0, T // U) as g:
        for j in range(U):
            hold(pe, s.diag, g * U + (t0 + j + 1), s.ticks_pe)
            mm(m.key_row[j].rearrange("p w c -> p (w c)"), m.ones[:, :],
               m.diag[:, j % 2, :, :].rearrange("p w c -> p (w c)"), start=True, stop=True).then_inc(s.key_row, 1)
        for j in range(U):
            t = g * U + (t0 + j)
            slot = j % 2
            hold(pe, s.cell, t + 1, s.ticks_pe)
            hold(pe, s.same, t + 1, s.ticks_pe)
            hold(pe, s.valued, t + 1, s.ticks_pe)
            for w in range(2):
                last = mm(m.joined[slot][:, w, :], m.same[:, slot, w, :], m.cell[:, slot, w, :], start=True, stop=True)
            last.then_inc(s.joined, 1)
            if not wide:
                hold(pe, s.hist_in, t + 1, s.ticks_pe)
                half = (B - B // 2) * EC
                flat = m.weighted[:, slot, :, :].rearrange("p b c -> p (b c)")
                mm(m.hist_dst[0], m.node_lo[:, slot, :], flat[:, 0:half], start=False, stop=True, skip_group_check=True)
                mm(m.hist_dst[1], m.node_lo[:, slot, :], flat[:, half:B * EC], start=False, stop=True, skip_group_check=True)
                mm(m.hist_src, m.cell[:, slot, 1, :], m.node_hi[:, slot, :], start=False, stop=True, skip_group_check=True).then_inc(
                    s.hist, 1)


def multiply(nc, pe, m, s, wide):
    mm = nc.tensor.matmul
    passes, last = plan(wide)
    ring = m.ring_wide if wide else m.ring_narrow
    evacuated = 0
    staged = loops = 0

    def product(done, i, p):
        step, _, n, posts = done
        index = i * n + (posts + p)
        wide_w = len(step["w"]) * D
        if step["w"] == ("ident",):
            w = m.ident[:, :]
        else:
            first = m.w_at[step["w"][0]]
            w = m.w[:, first:first + len(step["w"]), :].rearrange("p n d -> p (n d)")
        hold(pe, s.slot_ready, index + 1, s.ticks_pe)
        hold(pe, s.product_read, index + 1, s.ticks_pe)
        edge = step.get("edge")
        done_ = mm(m.product[:, 0:wide_w], m.sums_slot[:, :], w, start=True, stop=edge is None)
        if edge:
            fed = posts - EDGE_POSTS_BEFORE
            hold(pe, s.edge_ready, i * (16 * n) + 16 * (fed + p + 1), s.ticks_pe)
            done_ = mm(m.product[:, 0:D], m.edge_slot[:, :], m.w_edge[:, int(edge[1]), :], start=False, stop=True)
        done_.then_inc(s.product_ready, 1)

    for g, ps in enumerate(passes):
        step, width = ps["step"], ps["n"] * K * P
        pieces = cuts(width)
        table = m.narrow_table[step["xin"]]
        if g:
            evacuated += len(cuts(passes[g - 1]["n"] * K * P))
            pe.wait_ge(s.evacuated, evacuated)
        for c, n in pieces:
            mm(m.acc[:, c:c + n], m.zero_row[:, 0:P], m.zero_row[:, 0:n], start=True, stop=True,
               skip_group_check=True)
        if step["loop"]:
            pe.wait_ge(s.table_ready, ps["generation"] * B + min(B, ps["b0"] + ps["n"] * K))
            if wide:
                for j in range(K):
                    pe.wait_ge(s.staged, staged + j + 1)
                    mm(m.acc[:, j * P:(j + 1) * P], m.staged[:, j, :], m.ident[:, :], start=False,
                       stop=True, skip_group_check=True).then_inc(s.loops_used, 1)
                staged += K
            else:
                with pe.Fori(0, ps["n"] * K) as c:
                    for n in range(3):
                        mm(m.acc[:, bass.ds(c * P, P)],
                           table[:, bass.ds(c + ps["b0"], 1), n, :].rearrange("p o d -> p (o d)"),
                           m.ident_bf[:, :], start=False, stop=True, skip_group_check=True)
        with pe.Fori(0, K) as i:
            for j in range(K):
                hold(pe, s.rows_in[j], i * 16 + 16 * (g * K + 1), s.ticks_pe)
                if wide:
                    hold(pe, s.staged, i * K + (staged + j + 1), s.ticks_pe)
                    stationary = [m.staged[:, j, :]]
                else:
                    if ps["q"] == 0:
                        hold(pe, s.table_ready, i * K + (ps["generation"] * B + j + 1), s.ticks_pe)
                    stationary = [table[:, bass.ds(i * K + j, 1), n, :].rearrange("p o d -> p (o d)")
                                  for n in range(3)]
                for part in stationary:
                    for c, n in pieces:
                        last_mm = mm(m.acc[:, c:c + n], part, ring[:, j, c:c + n], start=False, stop=True, skip_group_check=True)
                last_mm.then_inc(s.rows_used, 1)
                if ps["done"] is not None and j in post_slots(ps["done"][2]):
                    product(ps["done"], i, post_slots(ps["done"][2]).index(j))
        if wide:
            staged += B
    with pe.Fori(0, K) as i:
        for p in range(last[2]):
            product(last, i, p)


EDGE_POSTS_BEFORE = B * next(n for n, step in enumerate(STEPS) if "edge" in step)


_INS = ["x", "src", "dst", "edge_attr_16", "L0_gnn_W_self", "L0_gnn_b_self", "L0_gnn_W_s2d", "L0_gnn_b_s2d",
        "L0_gnn_W_d2s", "L0_gnn_b_d2s", "L1_gnn_W1", "L1_gnn_b1", "L1_gnn_W2", "L1_gnn_b2", "L3_gnn_W0",
        "L3_gnn_b0", "L3_gnn_W1", "L3_gnn_b1", "L3_gnn_W2", "L3_gnn_b2", "L3_gnn_W3", "L3_gnn_b3"]


def arguments(t):
    w1, w2, w3 = t["L3_gnn_W1"], t["L3_gnn_W2"], t["L3_gnn_W3"]
    a = Names()
    a.x, a.src, a.dst, a.edge_attr, a.out = t["x"], t["src"], t["dst"], t["edge_attr_16"], t["out"]
    a.w_self = t["L0_gnn_W_self"]
    a.w = dict(s2d=t["L0_gnn_W_s2d"], d2s=t["L0_gnn_W_d2s"], g1=t["L1_gnn_W1"], g2=t["L1_gnn_W2"],
               e0=t["L3_gnn_W0"][0:D, :], e1=w1[0:D, :], e2a=w2[0:D, :], e2b=w2[D:2 * D, :],
               e3a=w3[0:D, :], e3b=w3[D:2 * D, :], e3c=w3[2 * D:3 * D, :])
    a.w_edge = [t["L3_gnn_W0"][D:D + EDGE_DIM, :], w1[D:D + EDGE_DIM, :], w2[2 * D:2 * D + EDGE_DIM, :],
                w3[3 * D:3 * D + EDGE_DIM, :]]
    a.b_edge = [t[f"L3_gnn_b{n}"] for n in range(4)]
    a.bias0 = [t["L0_gnn_b_self"], t["L0_gnn_b_s2d"], t["L0_gnn_b_d2s"]]
    a.bias1 = [t["L1_gnn_b1"], t["L1_gnn_b2"]]
    return a


def kernel(**inputs):
    import concourse.bacc as _bacc
    from concourse.bass_utils import run_bass_kernel_spmd as _run

    nc = _bacc.Bacc("TRN2", target_bir_lowering=False, num_devices=1)
    arrays, t = {}, {}
    for name in _INS:
        array = np.ascontiguousarray(inputs[name])
        arrays[f"in_{name}_dram"] = array
        t[name] = nc.dram_tensor(f"in_{name}_dram", array.shape, mybir.dt.from_np(array.dtype),
                                 kind="ExternalInput").ap()
    t["out"] = nc.dram_tensor("out_0_dram", (N, D), F32, kind="ExternalOutput").ap()
    build_gnn(nc, arguments(t))
    r = _run(nc, [arrays], core_ids=[0])
    return r.results[0]["out_0_dram"]
```

```python
from contextlib import ExitStack

import numpy as np
import concourse.bass as bass
from concourse import mybir

N = 6250
E = 106250
D = 128
EDGE_DIM = 16
EC = EDGE_DIM + 1
EPS = 1e-5

P = 128
B = -(-N // P)
NP = B * P
LAST = N - (B - 1) * P
T = 832
FULL = E // T
REST = E - FULL * T
U = 4
G = T // U
ROW = P + 2
K = 7
RING = 4
PAD = NP
ROWS = (B + 1) * P * B
SPARE = (NP + 1) * B + 1
EXACT = 256

F32 = mybir.dt.float32
F32R = mybir.dt.float32r
BF16 = mybir.dt.bfloat16
I32 = mybir.dt.int32
U32 = mybir.dt.uint32
ALU = mybir.AluOpType
ACT = mybir.ActivationFunctionType
AX = mybir.AxisListType.X

STEPS = [
    dict(into="dst", loop=False, w=("s2d",), post="add_scaled", xin=0, xout=None),
    dict(into="src", loop=False, w=("d2s",), post="layer0_end", xin=0, xout=1),
    dict(into="dst", loop=True, w=("g1",), post="gcn_hidden", xin=1, xout=0),
    dict(into="dst", loop=True, w=("g2",), post="layer1_end", xin=0, xout=1),
    dict(into="src", loop=True, w=("ident",), post="hop", xin=1, xout=0),
    dict(into="src", loop=True, w=("ident",), post="hop", xin=0, xout=1),
    dict(into="src", loop=True, w=("ident",), post="layer2_end", xin=1, xout=0),
    dict(into="dst", loop=False, w=("e0",), edge="e0", post="edge0", xin=0, xout=1),
    dict(into="dst", loop=False, w=("e1", "e2a", "e3a"), edge="e1", post="edge1", xin=1, xout=0),
    dict(into="dst", loop=False, w=("e2b", "e3b"), edge="e2", post="edge2", xin=0, xout=1),
    dict(into="dst", loop=False, w=("e3c",), edge="e3", post="edge3", xin=1, xout=None),
]
NORM_LINKS = 5
POST_LINKS = dict(add_scaled=1, layer0_end=2 + NORM_LINKS, gcn_hidden=2, layer1_end=3 + NORM_LINKS, hop=1,
                  layer2_end=2 + NORM_LINKS, edge0=1, edge1=3, edge2=3, edge3=1)


NORMED_BEFORE = {"layer0_end": B, "layer1_end": 2 * B, "layer2_end": 3 * B}


def post_links(step):
    return POST_LINKS[step["post"]] + (1 if step["xout"] is not None else 0)


def back(j):
    return min(d for d in range(1, K + 1) if (j - d) % K % RING == j % RING)


def plan(wide):
    widths = [1] * K if wide else [2, 2, 2, 1]
    passes, posts, done, generation, used = [], 0, None, 0, 0
    for step in STEPS:
        b0 = 0
        for q, n in enumerate(widths):
            if step["loop"]:
                used += K * n
            passes.append(dict(step=step, q=q, b0=b0, n=n, done=done, generation=generation, used=used))
            used += B
            if done is not None:
                posts += K * done[2]
            done = (step, b0, n, posts)
            b0 += K * n
        if step["xout"] is not None:
            generation += 1
    return passes, done


def rows_count(g, i, j):
    of = sum(1 for other in range(K) if other % RING == j % RING)
    return i * (16 * of) + 16 * (of * K * g + j // RING + 1)


def split(width):
    return 512 * round(width * 0.55 / 512)


def cuts(width):
    return [(c, min(512, width - c)) for c in range(0, width, 512)]


class Names:
    pass


def build_gnn(nc, a):
    ctx = ExitStack()
    with ctx:
        def sb(name, shape, dt=F32):
            return ctx.enter_context(nc.sbuf_tensor(name, shape, dt))

        def sem(name):
            return ctx.enter_context(nc.semaphore(name))

        m = Names()
        m.wide_of, m.narrow_of = {}, {}
        for into in ("dst", "src"):
            w = nc.dram_tensor(f"counts_into_{into}", (ROWS, P), F32, kind="Internal").ap()
            m.wide_of[into] = w
            m.narrow_of[into] = w.bitcast(BF16).rearrange("r (h c) -> (r h) c", h=2)[0:ROWS, :]
        m.edge_sums_dram = nc.dram_tensor("edge_sums_t", (EC, NP), F32, kind="Internal").ap()

        m.x = sb("x", [P, B, D])
        table0 = sb("table0", [P, B * D])
        arena = sb("arena", [P, T * EDGE_DIM + 6 * T + NP // 4])
        cut = [0]

        def part(n):
            cut[0] += n
            assert cut[0] <= arena.shape[1]
            return arena[:, cut[0] - n:cut[0]]

        table1 = part(B * D)
        m.table = [t.rearrange("p (b d) -> p b d", b=B) for t in (table0[:, :], table1)]
        m.carry = part(B * D).rearrange("p (b d) -> p b d", b=B)
        ring = part(RING * K * P)
        m.ring_narrow = ring.bitcast(BF16).rearrange("p (j n) -> p j n", j=RING)
        m.ring_wide = ring.rearrange("p (j n) -> p j n", j=RING)
        m.sums_t = part(2 * K * P)
        m.staged_wide = part(RING * D).rearrange("p (j d) -> p j d", j=RING)
        m.edge_sums_t = table1[0:EC, 0:NP]
        cut[0] = 0
        m.attr = part(T * EDGE_DIM).rearrange("p (t c) -> p t c", c=EDGE_DIM)
        m.key = part(2 * T).rearrange("p (t w) -> p t w", w=2)
        m.lo = part(T).bitcast(BF16).rearrange("p (t w) -> p t w", w=2)
        m.hi = part(T).bitcast(BF16).rearrange("p (t w) -> p t w", w=2)
        m.zeros = part(NP // 4)
        raw = part(2 * T)
        m.raw = raw.bitcast(I32).rearrange("p (w t) -> p w t", w=2)
        cut[0] -= 2 * T
        m.key_cols = part(2 * U).rearrange("p (j w) -> p j w", w=2)
        m.lo_cols = part(2 * U).rearrange("p (j w) -> p j w", w=2)
        m.hi_cols = part(2 * U).rearrange("p (j w) -> p j w", w=2)
        m.attr_cols = part(U * EDGE_DIM).rearrange("p (j c) -> p j c", c=EDGE_DIM)
        values = part(2 * U * ROW)
        m.values_wide = values.rearrange("p (j w c) -> p j w c", j=U, w=2)
        m.values = values[:, 0:U * ROW].bitcast(BF16).rearrange("p (j w c) -> p j w c", j=U, w=2)
        m.rows_r = sb("rows_r", [P, RING, 2 * K * P], F32R)
        m.staged_r = sb("staged_r", [P, RING, 2, D], F32R)
        m.ident_r = sb("ident_r", [P, P], F32R)
        m.index = sb("index", [P, 2 * U], U32)
        m.diag = sb("diag", [P, 2, 2, P])
        m.same = sb("same", [P, 2, 2, 2, 2 * P], BF16)
        m.cell = sb("cell", [P, 2, 2, 2, ROW], BF16)
        m.mark = sb("mark", [P, 2], I32)
        m.limit = sb("limit", [P, 2, 2, 2])
        m.late = sb("late", [P, 2, 2, 2])
        m.spare_late = sb("spare_late", [P, 2, 2, 2])
        m.late_row = sb("late_row", [P, 2, 2])
        m.node_lo = sb("node_lo", [P, 2, 2, P])
        m.node_hi = sb("node_hi", [P, 2, 2, 2, B], BF16)
        m.weighted = sb("weighted", [P, 2, 2, B, EDGE_DIM])

        m.ident = sb("ident", [P, P])
        m.ones = sb("ones", [P, P])
        m.iota = sb("iota", [P, P])
        m.iota_i = sb("iota_i", [P, P], I32)
        m.spare_i = sb("spare_i", [P, 2], I32)
        m.spare = sb("spare", [P, 2, 4])
        m.nought = sb("nought", [P, P], BF16)

        m.w_self = sb("w_self", [P, D])
        m.w = sb("w", [P, 11, D])
        names = ("s2d", "d2s", "g1", "g2", "e0", "e1", "e2a", "e3a", "e2b", "e3b", "e3c")
        m.w_at = {name: n for n, name in enumerate(names)}
        m.w_edge = sb("w_edge", [EC, 4, D])
        m.bias0 = sb("bias0", [1, 3, D])
        m.bias0_sum = sb("bias0_sum", [1, D])
        m.bias1 = sb("bias1", [P, 2, D])

        m.edge_sums = sb("edge_sums", [P, B, EC])
        m.n_src = sb("n_src", [P, B])
        m.scale = {k: sb(k, [P, B]) for k in ("inv_dst", "inv_src", "half_inv_dst", "half_inv_src",
                                              "dis_dst", "dis_src", "dis2_src")}
        m.most = sb("most", [P, 3])
        m.flag = sb("flag", [1, 4], I32)

        m.sums_slot = sb("sums_slot", [P, P])
        m.edge_slot = sb("edge_slot", [EC, P])
        m.edge_block = sb("edge_block", [P, EC])
        m.xn = sb("xn", [P, D])
        m.stats = sb("stats", [P, 6])
        m.meanvar = sb("meanvar", [P, 2])
        m.std = sb("std", [P, 1])
        m.rstd = sb("rstd", [P, 1])
        m.eps = sb("eps", [P, 1])
        m.nil = sb("nil", [P, 1])
        m.root = {end: sb(f"root_{end}", [P, B]) for end in ("dst", "src")}
        m.v = sb("v", [P, D])
        m.r = sb("r", [P, D])
        m.vt = sb("vt", [P, D])

        psum = ctx.enter_context(nc.psum_tensor("psum", [P, 8, 512], F32))
        m.acc = psum[:, 0:4, :].rearrange("p b n -> p (b n)")
        m.product = psum[:, 4, :]
        m.hist_dst = [psum[:, 0, 0:(B - B // 2) * EDGE_DIM], psum[:, 1, 0:(B // 2) * EDGE_DIM]]
        m.hist_banks = [psum[:, 0, :], psum[:, 1, :]]
        m.edges_of = [psum[:, 1, 512 - 2 * B:512 - B], psum[:, 1, 512 - B:512]]
        m.joined = [psum[:, 2 + j, 0:2 * ROW].rearrange("p (w c) -> p w c", w=2) for j in range(2)]
        m.key_row = [psum[:, 4 + q, :].rearrange("p (w c) -> p w c", w=2) for q in range(2)]
        m.edge_row = psum[:, 6, :]

        s = Names()
        s.edges_in = sem("edges_in")
        s.cols_own = sem("cols_own")
        s.blocks = sem("blocks")
        s.lo = sem("lo")
        s.cell = sem("cell")
        s.most = sem("most")
        s.most_row = sem("most_row")
        s.zeroed = sem("zeroed")
        s.landed = sem("landed")
        s.var = sem("var")
        s.std = sem("std")
        s.degree = sem("degree")
        s.root = sem("root")
        s.attr_in = sem("attr_in")
        s.x_in = sem("x_in")
        s.weights_in = sem("weights_in")
        s.consts = sem("consts")
        s.pads = sem("pads")
        s.zeros_set = sem("zeros_set")
        s.cols = sem("cols")
        s.diag = sem("diag")
        s.key_row = sem("key_row")
        s.same = sem("same")
        s.indexed = sem("indexed")
        s.joined = sem("joined")
        s.valued = sem("valued")
        s.hist_in = sem("hist_in")
        s.hist = sem("hist")
        s.flag_ready = sem("flag_ready")
        s.chain = sem("chain")
        s.pre_v = sem("pre_v")
        s.pre_t = sem("pre_t")
        s.pre_vt = sem("pre_vt")
        s.pre_done = sem("pre_done")
        s.edge_blk = sem("edge_blk")
        s.edge_t = sem("edge_t")
        s.edge_out = sem("edge_out")
        s.edge_stored = sem("edge_stored")
        s.into_dst = sem("into_dst")
        s.into_src = sem("into_src")
        s.wide_dst = sem("wide_dst")
        s.wide_src = sem("wide_src")
        s.used = sem("used")
        s.cast_act = sem("cast_act")
        s.cast_dve = sem("cast_dve")
        s.evac_act = sem("evac_act")
        s.evac_dve = sem("evac_dve")
        s.halved = sem("halved")
        s.table_ready = sem("table_ready")
        s.slot_ready = sem("slot_ready")
        s.edge_ready = sem("edge_ready")
        s.product_ready = sem("product_ready")
        s.product_read = sem("product_read")
        s.staged = sem("staged")
        s.final = sem("final")
        s.out_stored = sem("out_stored")
        s.ticks_pe = sem("ticks_pe")
        s.ticks_act = sem("ticks_act")
        s.ticks_dve = sem("ticks_dve")
        s.ticks_pool = sem("ticks_pool")
        s.rows_in = [sem(f"rows_in_{j}") for j in range(RING)]
        s.spare_narrow, s.spare_wide = 2 * 16, 4 * 16

        block = ctx.enter_context(nc.Block())
        sync_program(nc, block, a, m, s)
        pool_program(nc, block, a, m, s)
        scalar_program(nc, block, a, m, s)
        vector_program(nc, block, a, m, s)
        tensor_program(nc, block, a, m, s)


def hold(eng, sem, value, ticks):
    eng.wait_ge(sem, value)
    eng.sem_inc(ticks, 1)


def rows_of(m, into, wide):
    flat = (m.wide_of if wide else m.narrow_of)[into]
    return flat.rearrange("(n b) c -> n (b c)", b=B)


def sync_program(nc, block, a, m, s):
    @block.sync
    def _(sp):
        sp.wait_ge(s.pads, 1)
        for w, ends in ((0, a.dst), (1, a.src)):
            sp.dma_start(m.raw[0:FULL, w, :], ends[0:FULL * T].rearrange("(p t) -> p t", t=T)).then_inc(s.edges_in, 16)
            sp.dma_start(m.raw[FULL:FULL + 1, w, 0:REST],
                         ends[FULL * T:E].rearrange("(p t) -> p t", p=1)).then_inc(s.edges_in, 16)
        sp.wait_ge(s.pads, 2)
        for b in range(0, B - 1, 16):
            sp.dma_start(m.x[:, b:b + 16, :], a.x[b * P:(b + 16) * P, :].rearrange("(b p) d -> p b d", p=P)).then_inc(
                s.x_in, 16)
        sp.dma_start(m.x[0:LAST, B - 1, :], a.x[(B - 1) * P:N, :]).then_inc(s.x_in, 16)
        for w in ("s2d", "d2s", "g1", "g2", "e0", "e1", "e2a", "e3a", "e2b", "e3b", "e3c"):
            sp.dma_start(m.w[:, m.w_at[w], :], a.w[w]).then_inc(s.weights_in, 16)
        sp.dma_start(m.w_self[:, :], a.w_self).then_inc(s.weights_in, 16)
        for n in range(4):
            sp.dma_start(m.w_edge[0:EDGE_DIM, n, :], a.w_edge[n]).then_inc(s.weights_in, 16)
            sp.dma_start(m.w_edge[EDGE_DIM:EC, n, :], a.b_edge[n].rearrange("(o d) -> o d", o=1)).then_inc(
                s.weights_in, 16)
        for n in range(3):
            sp.dma_start(m.bias0[0:1, n, :], a.bias0[n].rearrange("(o d) -> o d", o=1)).then_inc(s.weights_in, 16)
        for n in range(2):
            sp.dma_start(m.bias1[:, n, :], a.bias1[n].rearrange("(o d) -> o d", o=1).broadcast_to([P, D])).then_inc(
                s.weights_in, 16)
        sp.wait_ge(s.pads, 3)
        whole = T * EDGE_DIM
        attr = m.attr.rearrange("p t c -> p (t c)")
        source = a.edge_attr.rearrange("e c -> (e c)")
        for p0, p1 in ((0, 112), (112, FULL)):
            sp.dma_start(attr[p0:p1, :], source[p0 * whole:p1 * whole].rearrange("(p t) -> p t", t=whole)).then_inc(
                s.attr_in, 16)
        sp.dma_start(attr[FULL:FULL + 1, 0:REST * EDGE_DIM],
                     source[FULL * whole:].rearrange("(p t) -> p t", p=1)).then_inc(s.attr_in, 16)
        sp.wait_ge(s.zeros_set, 1)
        fill_zeros(sp, m, s, False)
        sp.wait_ge(s.edge_out, B)
        sp.dma_start(m.edge_sums_dram, m.edge_sums_t[:, :]).then_inc(s.edge_stored, 16)

        sp.wait_ge(s.flag_ready, 1)
        wide = sp.value_load(m.flag[0:1, 0:1])
        with sp.If(wide == 1):
            sp.wait_ge(s.into_dst, s.spare_narrow + 16 * T)
            sp.wait_ge(s.into_src, s.spare_narrow + 16 * T)
            sp.wait_ge(s.zeros_set, 2)
            fill_zeros(sp, m, s, True)
            stream_rows(sp, a, m, s, True)
        with sp.Else():
            stream_rows(sp, a, m, s, False)
        sp.wait_ge(s.out_stored, 2 * 16)


def fill_zeros(sp, m, s, wide):
    zeros = m.zeros if wide else m.zeros.bitcast(BF16)
    n = zeros.shape[1]
    for into in ("dst", "src"):
        rows = rows_of(m, into, wide)
        with sp.Fori(0, B) as b:
            for c in range(0, NP, n):
                sp.dma_start(rows[bass.ds(b * P, P), c:c + n], zeros).then_inc(s.zeroed, 16)


def stream_rows(sp, a, m, s, wide):
    passes, _ = plan(wide)
    ring = m.ring_wide if wide else m.ring_narrow
    start = (s.spare_wide if wide else s.spare_narrow) + 16 * T
    sp.wait_ge(s.wide_dst if wide else s.into_dst, start)
    sp.wait_ge(s.wide_src if wide else s.into_src, start)
    sp.wait_ge(s.edge_stored, 16)
    for g, ps in enumerate(passes):
        rows = rows_of(m, ps["step"]["into"], wide)
        width = ps["n"] * K * P
        with sp.Fori(0, K) as i:
            for j in range(K):
                free = K - back(j) + j + 1
                if wide:
                    sp.wait_ge(s.used, i * K + (ps["used"] + free))
                else:
                    sp.wait_ge(s.cast_act, i * K + (g * B + free))
                    sp.wait_ge(s.cast_dve, i * K + (g * B + free))
                sp.dma_start(ring[:, j % RING, 0:width],
                             rows[bass.ds(i * (K * P) + j * P, P), ps["b0"] * P:ps["b0"] * P + width]).then_inc(
                                 s.rows_in[j % RING], 16)
    sp.wait_ge(s.final, B)
    sp.dma_start(a.out[0:(B - 1) * P, :].rearrange("(b p) d -> p b d", p=P), m.x[:, 0:B - 1, :]).then_inc(
        s.out_stored, 16)
    sp.dma_start(a.out[(B - 1) * P:N, :], m.x[0:LAST, B - 1, :]).then_inc(s.out_stored, 16)


def pool_program(nc, block, a, m, s):
    @block.gpsimd
    def _(pool):
        pool.memset(m.raw, PAD).then_inc(s.pads, 1)
        pool.memset(m.x[:, B - 1, :], 0.0).then_inc(s.pads, 1)
        pool.memset(m.attr[:, REST:T, :], 0.0).then_inc(s.pads, 1)
        pool.iota(m.iota_i[:, :], pattern=[[1, P]], base=0, channel_multiplier=0).then_inc(s.consts, 1)
        pool.iota(m.spare_i[:, :], pattern=[[P, 2]], base=SPARE, channel_multiplier=1).then_inc(s.consts, 1)
        pool.iota(m.mark[:, 0:1], pattern=[[0, 1]], base=190 << 23, channel_multiplier=-(1 << 23)).then_inc(
            s.consts, 1)
        pool.iota(m.mark[:, 1:2], pattern=[[0, 1]], base=191 << 23, channel_multiplier=-(1 << 23)).then_inc(
            s.consts, 1)
        pool.memset(m.cell[:, :, :, :, P:ROW], 0.0).then_inc(s.consts, 1)
        pool.memset(m.limit[:, :, :, :], 0.0).then_inc(s.consts, 1)
        pool.memset(m.ones[:, :], 1.0).then_inc(s.consts, 1)
        pool.memset(m.nought[:, :], 0.0).then_inc(s.consts, 1)
        pool.memset(m.eps[:, :], EPS).then_inc(s.consts, 1)
        pool.memset(m.nil[:, :], 0.0).then_inc(s.consts, 1)
        pool.wait_ge(s.consts, 10)
        pool.affine_select(out=m.ident[:, :], in_=m.ones[:, :], compare_op=ALU.is_equal, fill=0.0,
                           base=0, pattern=[[-1, P]], channel_multiplier=1).then_inc(s.consts, 1)
        pool.wait_ge(s.consts, 11)
        pool.tensor_copy(m.ident_r[:, :], m.ident[:, :]).then_inc(s.consts, 1)
        pool.sem_inc(s.landed, 2)
        add_edges(pool, m, s, False)

        pool.wait_ge(s.flag_ready, 1)
        wide = pool.value_load(m.flag[0:1, 0:1])
        with pool.If(wide == 1):
            add_edges(pool, m, s, True)
            feed_blocks(pool, m, s, True)
        with pool.Else():
            feed_blocks(pool, m, s, False)


def add_edges(pool, m, s, wide):
    values = m.values_wide if wide else m.values
    done = (s.wide_dst, s.wide_src) if wide else (s.into_dst, s.into_src)
    flat = m.wide_of if wide else m.narrow_of
    before = T if wide else 0
    zeros = m.zeros if wide else m.zeros.bitcast(BF16)
    n = zeros.shape[1]
    spare = 16 * (NP // n)
    pool.wait_ge(s.zeros_set, 2 if wide else 1)
    if wide:
        pool.wait_ge(s.into_dst, s.spare_narrow + 16 * T)
        pool.wait_ge(s.into_src, s.spare_narrow + 16 * T)
    for w, into in enumerate(("dst", "src")):
        for c in range(0, NP, n):
            pool.dma_start(rows_of(m, into, wide)[B * P:(B + 1) * P, c:c + n], zeros).then_inc(done[w], 16)
    pool.wait_ge(s.zeroed, 2 * B * (s.spare_narrow + (s.spare_wide if wide else 0)))
    with pool.Fori(0, G) as g:
        for q in range(2):
            hold(pool, s.valued, g * U + (before + 2 * q + 4), s.ticks_pool)
            hold(pool, s.indexed, g * 2 + (before // 2 + q + 1), s.ticks_pool)
            for w, into in enumerate(("dst", "src")):
                hold(pool, done[w], g * (16 * U) + (spare + 32 * q), s.ticks_pool)
                if into == "src":
                    pool.sem_inc(s.landed, 1)
                for j in (2 * q, 2 * q + 1):
                    pool.indirect_dma_start(
                        out=flat[into], out_offset=bass.IndirectOffsetOnAxis(ap=m.index[:, 2 * j + w:2 * j + w + 1], axis=0),
                        in_=values[:, j, w, 0:P], in_offset=None, compute_op=ALU.add).then_inc(done[w], 16)


def feed_blocks(pool, m, s, wide):
    passes, last = plan(wide)

    def feed(done, i, p):
        _, b0, n, posts = done
        hold(pool, s.product_ready, i * n + (posts + p + 1), s.ticks_pool)
        pool.dma_start(m.edge_slot[:, :], m.edge_sums_dram[:, bass.ds(i * (n * P) + (b0 + p) * P, P)]).then_inc(
            s.edge_ready, 16)

    def stage(ps, i, b0, j, used):
        slot = j % RING
        hold(pool, s.table_ready, i * K + (ps["generation"] * B + b0 + j + 1), s.ticks_pool)
        hold(pool, s.used, i * K + (used + K - back(j) + j + 1), s.ticks_pool)
        block = one(m.table[ps["step"]["xin"]], i * K + (b0 + j))
        if wide:
            pool.tensor_copy(m.staged_wide[:, slot, :], block).then_inc(s.staged, 1)
        else:
            pool.tensor_copy(m.staged_r[:, slot, 0, :], block).then_inc(s.halved, 1)
            hold(pool, s.halved, i * K + (used + j + 1), s.ticks_pool)
            pool.tensor_tensor(m.staged_r[:, slot, 1, :], block, m.staged_r[:, slot, 0, :].bitcast(F32),
                               op=ALU.subtract).then_inc(s.staged, 1)

    pool.wait_ge(s.edge_stored, 16)
    for ps in passes:
        done = ps["done"]
        feeds = done is not None and "edge" in done[0]
        if ps["step"]["loop"]:
            with pool.Fori(0, ps["n"]) as i:
                for j in range(K):
                    stage(ps, i, ps["b0"], j, ps["used"] - ps["n"] * K)
        with pool.Fori(0, K) as i:
            for j in range(K):
                if feeds and j in product_at(done[2]):
                    feed(done, i, product_at(done[2]).index(j))
                stage(ps, i, 0, j, ps["used"])
    with pool.Fori(0, K) as i:
        for p in range(last[2]):
            feed(last, i, p)


def product_at(n):
    return [0, 3][0:n]


def finish_at(n):
    return [3, 6][0:n]


def scalar_program(nc, block, a, m, s):
    @block.scalar
    def _(act):
        act.wait_ge(s.consts, 12)
        act.sem_inc(s.valued, 2)
        with act.Fori(0, B) as b:
            deviation(nc, act, m, s, b)
            hold(act, s.pre_t, b + 1, s.ticks_act)
            nc.scalar.copy(m.vt[:, :], m.product[:, 0:P]).then_inc(s.pre_vt, 1)
        spread_keys(nc, act, m, s, False)
        act.wait_ge(s.degree, 2)
        for end in ("dst", "src"):
            nc.scalar.activation(m.root[end][:, :], m.scale[f"dis_{end}"][:, :], ACT.Sqrt, bias=m.nil[:, :]).then_inc(
                s.root, 1)
        with act.Fori(0, B) as b:
            hold(act, s.edge_t, b + 1, s.ticks_act)
            nc.scalar.copy(m.edge_sums_t[:, bass.ds(b * P, P)], m.edge_row[0:EC, 0:P]).then_inc(s.edge_out, 1)

        act.wait_ge(s.flag_ready, 1)
        wide = act.value_load(m.flag[0:1, 0:1])
        with act.If(wide == 1):
            act.wait_ge(s.into_dst, s.spare_narrow + 16 * T)
            act.wait_ge(s.into_src, s.spare_narrow + 16 * T)
            spread_keys(nc, act, m, s, True)
            hand_over_sums(nc, act, m, s, True)
        with act.Else():
            hand_over_sums(nc, act, m, s, False)


def deviation(nc, act, m, s, index):
    hold(act, s.var, index + 1, s.ticks_act)
    nc.scalar.activation(m.std[:, :], m.meanvar[:, 1:2], ACT.Sqrt, bias=m.eps[:, :]).then_inc(s.std, 1)


def spread_keys(nc, act, m, s, wide):
    values = m.values_wide if wide else m.values
    t0 = T if wide else 0
    with act.Fori(0, T // U) as g:
        hold(act, s.cols, g + (t0 // U + 1), s.ticks_act)
        for j in range(U):
            if j >= 2:
                hold(act, s.key_row, g * U + (t0 + j - 1), s.ticks_act)
            for w in range(2):
                last = nc.scalar.activation(m.diag[:, j % 2, w, :], m.ident[:, :], ACT.Copy,
                                            scale=m.key_cols[:, j, w:w + 1])
            last.then_inc(s.diag, 1)
        for q in range(2):
            if not wide:
                hold(act, s.cell, g * 2 + (t0 // 2 + q + 1), s.ticks_act)
                nc.scalar.copy(m.node_lo[:, q, :, :], m.cell[:, q, :, 0, 0:P]).then_inc(s.lo, 1)
            hold(act, s.landed, g * 2 + (t0 // 2 + q + 2), s.ticks_act)
            for tile in range(2):
                j = 2 * q + tile
                hold(act, s.joined, g * U + (t0 + j + 5), s.ticks_act)
                nc.scalar.copy(values[:, j, :, :], m.joined[tile]).then_inc(s.valued, 1)


def hand_over_sums(nc, act, m, s, wide):
    passes, last = plan(wide)
    evacuated = [0, 0]

    def slot(done, i, p):
        _, b0, n, posts = done
        hold(act, s.product_ready, i * n + (posts + p + 1), s.ticks_act)
        nc.scalar.copy(m.sums_slot[:, :], m.sums_t[:, bass.ds(i * (n * P) + p * P, P)]).then_inc(s.slot_ready, 1)

    def root(done, i, p):
        step, b0, n, _ = done
        if step["post"] in NORMED_BEFORE:
            deviation(nc, act, m, s, i * n + (b0 + p + NORMED_BEFORE[step["post"]]))

    for g, ps in enumerate(passes):
        done, width = ps["done"], ps["n"] * K * P
        n = done[2] if done else 0
        act.wait_ge(s.evac_act, evacuated[0]) if g else None
        act.wait_ge(s.evac_dve, evacuated[1]) if g else None
        if not (wide and done is None):
            with act.Fori(0, K) as i:
                for j in range(K):
                    if not wide:
                        cast(act, m, s, ps, g, i, j, width, False, s.ticks_act)
                    if done and j in finish_at(n):
                        root(done, i, finish_at(n).index(j))
                    if done and j in product_at(n):
                        slot(done, i, product_at(n).index(j))
        act.wait_ge(s.used, K + ps["used"] + B)
        for c, (at, size) in enumerate(cuts(width)):
            if c % 2 == 0:
                nc.scalar.copy(m.sums_t[:, at:at + size], m.acc[:, at:at + size]).then_inc(s.evac_act, 1)
            evacuated[c % 2] += 1
    act.wait_ge(s.evac_act, evacuated[0])
    act.wait_ge(s.evac_dve, evacuated[1])
    with act.Fori(0, K) as i:
        for p in range(last[2]):
            slot(last, i, p)
            root(last, i, p)


def cast(eng, m, s, ps, g, i, j, width, by_vector, ticks):
    slot = j % RING
    hold(eng, s.rows_in[slot], rows_count(g, i, j), ticks)
    hold(eng, s.used, i * K + (ps["used"] + K - back(j) + j + 1), ticks)
    at = split(width)
    if by_vector:
        eng.tensor_copy(m.rows_r[:, slot, at:width], m.ring_narrow[:, slot, at:width]).then_inc(s.cast_dve, 1)
    else:
        eng.copy(m.rows_r[:, slot, 0:at], m.ring_narrow[:, slot, 0:at]).then_inc(s.cast_act, 1)


class Chain:

    def __init__(self, dve, sem):
        self.dve, self.sem, self.base, self.at, self.turn, self.each = dve, sem, 0, 0, None, 0

    def enter(self, turn, each):
        self.turn, self.each, self.at = turn, each, 0

    def leave(self, rounds):
        assert self.at == self.each, (self.at, self.each)
        self.base += rounds * self.each
        self.turn = None

    def link(self, instruction):
        instruction.then_inc(self.sem, 1)
        if self.turn is None:
            self.base += 1
            self.dve.wait_ge(self.sem, self.base)
        else:
            self.at += 1
            self.dve.wait_ge(self.sem, self.turn * self.each + (self.base + self.at))


def one(tensor, b):
    return tensor[:, bass.ds(b, 1), :].rearrange("p o d -> p (o d)")


def normalize(nc, dve, chain, m, s, index, scale=None):
    v = nc.vector
    chain.link(v.bn_stats(m.stats[:, :], m.xn[:, :]))
    dve.sem_inc(s.ticks_dve, 1)
    chain.link(v.bn_aggr(m.meanvar[:, :], m.stats[:, :]))
    dve.sem_inc(s.var, 1)
    hold(dve, s.std, index + 1, s.ticks_dve)
    chain.link(v.reciprocal(m.rstd[:, :], m.std[:, :]))
    chain.link(v.tensor_scalar(m.r[:, :], m.xn[:, :], m.meanvar[:, 0:1], m.rstd[:, :],
                               op0=ALU.subtract, op1=ALU.mult))
    if scale is None:
        chain.link(v.tensor_scalar(m.v[:, :], m.r[:, :], 0.0, None, op0=ALU.max))
    else:
        chain.link(v.tensor_scalar(m.v[:, :], m.r[:, :], 0.0, scale, op0=ALU.max, op1=ALU.mult))


def write_table(nc, dve, chain, m, s, table, b):
    chain.link(nc.vector.tensor_scalar(one(m.table[table], b), m.v[:, :], 1.0, None, op0=ALU.mult))
    dve.sem_inc(s.table_ready, 1)


def vector_program(nc, block, a, m, s):
    @block.vector
    def _(dve):
        v = nc.vector
        chain = Chain(dve, s.chain)
        dve.wait_ge(s.consts, 12)
        chain.link(v.tensor_copy(m.iota[:, :], m.iota_i[:, :]))
        chain.link(v.tensor_copy(m.spare[:, :, :], m.spare_i[:, :].unsqueeze(2).broadcast_to([P, 2, 4])))
        mark = m.mark[:, :].bitcast(F32)
        for tile in range(2):
            for pair in range(2):
                chain.link(v.tensor_copy(m.cell[:, pair, tile, :, P + tile], mark[:, 0:1].broadcast_to([P, 2])))
            chain.link(v.tensor_copy(m.limit[:, tile, :, tile], mark[:, 1:2].broadcast_to([P, 2])))
        chain.link(v.memset(m.limit[:, 0, :, 1], 3e38))
        dve.wait_ge(s.pads, 3)
        v.memset(m.zeros, 0.0).then_inc(s.zeros_set, 1)

        dve.wait_ge(s.edges_in, 4 * 16)
        whole = m.key.rearrange("p t w -> p (t w)").bitcast(I32).rearrange("p (w t) -> p w t", w=2)
        chain.link(v.tensor_single_scalar(whole, m.raw, P - 1, op=ALU.bitwise_and))
        chain.link(v.tensor_copy(m.lo.rearrange("p t w -> p w t"), whole))
        chain.link(v.tensor_single_scalar(whole, m.raw, 7, op=ALU.logical_shift_right))
        chain.link(v.tensor_copy(m.hi.rearrange("p t w -> p w t"), whole))
        for w in range(2):
            chain.link(v.scalar_tensor_tensor(m.key[:, :, w], m.hi[:, :, 1 - w], float(P), m.lo[:, :, 1 - w],
                                              op0=ALU.mult, op1=ALU.add))
            chain.link(v.scalar_tensor_tensor(m.key[:, :, w], m.key[:, :, w], float(B), m.hi[:, :, w],
                                              op0=ALU.mult, op1=ALU.add))

        dve.wait_ge(s.x_in, 4 * 16)
        dve.wait_ge(s.weights_in, 25 * 16)
        chain.link(v.tensor_tensor(m.bias0_sum[:, :], m.bias0[:, 1, :], m.bias0[:, 2, :], op=ALU.add))
        chain.link(v.scalar_tensor_tensor(m.bias0_sum[:, :], m.bias0_sum[:, :], 0.5, m.bias0[:, 0, :],
                                          op0=ALU.mult, op1=ALU.add))
        with dve.Fori(0, B) as b:
            chain.enter(b, 1 + NORM_LINKS + 1 + 1)
            chain.link(v.tensor_scalar(m.xn[:, :], one(m.x, b), 1.0, None, op0=ALU.mult))
            normalize(nc, dve, chain, m, s, b)
            dve.sem_inc(s.pre_v, 1)
            write_table(nc, dve, chain, m, s, 0, b)
            hold(dve, s.pre_done, b + 1, s.ticks_dve)
            chain.link(v.tensor_tensor(one(m.x, b), m.product[:, 0:D], one(m.x, b), op=ALU.add))
        chain.leave(B)

        dve.wait_ge(s.attr_in, 3 * 16)
        index_edges(nc, dve, chain, m, s, False)

        dve.wait_ge(s.hist, T // 2 + 2)
        half = B - B // 2
        for (b0, b1), sums in zip(((0, half), (half, B)), m.hist_dst):
            chain.link(v.tensor_copy(m.edge_sums[:, b0:b1, 0:EDGE_DIM], sums.rearrange("p (b c) -> p b c", c=EDGE_DIM)))
        chain.link(v.tensor_copy(m.edge_sums[:, :, EDGE_DIM], m.edges_of[0]))
        chain.link(v.tensor_copy(m.n_src[:, :], m.edges_of[1]))
        n_dst = m.edge_sums[:, :, EDGE_DIM]
        for end, n in (("dst", n_dst), ("src", m.n_src[:, :])):
            inv, half_inv = m.scale[f"inv_{end}"][:, :], m.scale[f"half_inv_{end}"][:, :]
            chain.link(v.tensor_scalar(inv, n, 1.0, None, op0=ALU.max))
            chain.link(v.reciprocal(inv, inv))
            chain.link(v.tensor_scalar(half_inv, inv, 0.5, None, op0=ALU.mult))
            chain.link(v.tensor_scalar(m.scale[f"dis_{end}"][:, :], n, 1.0, None, op0=ALU.add))
            dve.sem_inc(s.degree, 1)
        dve.wait_ge(s.root, 2)
        for end in ("dst", "src"):
            chain.link(v.reciprocal(m.scale[f"dis_{end}"][:, :], m.root[end][:, :]))
        chain.link(v.tensor_tensor(m.scale["dis2_src"][:, :], m.scale["dis_src"][:, :], m.scale["dis_src"][:, :],
                                   op=ALU.mult))
        chain.link(v.tensor_reduce(out=m.most[:, 0:1], in_=n_dst, axis=AX, op=ALU.max))
        chain.link(v.tensor_reduce(out=m.most[:, 1:2], in_=m.n_src[:, :], axis=AX, op=ALU.max))
        v.tensor_tensor(m.most[:, 2:3], m.most[:, 0:1], m.most[:, 1:2], op=ALU.max).then_inc(s.most, 1)
        dve.wait_ge(s.most_row, 1)
        chain.link(v.tensor_reduce(out=m.rstd[0:1, 0:1], in_=m.product[0:1, 0:P], axis=AX, op=ALU.max))
        v.tensor_scalar(m.flag[0:1, 0:1], m.rstd[0:1, 0:1], float(EXACT), None, op0=ALU.is_gt).then_inc(
            s.flag_ready, 1)
        with dve.Fori(0, B) as b:
            v.tensor_scalar(m.edge_block[:, :], one(m.edge_sums, b), 1.0, None, op0=ALU.mult).then_inc(s.edge_blk, 1)
            hold(dve, s.edge_out, b + 1, s.ticks_dve)

        dve.wait_ge(s.flag_ready, 1)
        wide = dve.value_load(m.flag[0:1, 0:1])
        before = chain.base
        with dve.If(wide == 1):
            dve.wait_ge(s.edge_stored, 16)
            v.memset(m.zeros, 0.0).then_inc(s.zeros_set, 1)
            dve.wait_ge(s.into_dst, s.spare_narrow + 16 * T)
            dve.wait_ge(s.into_src, s.spare_narrow + 16 * T)
            index_edges(nc, dve, chain, m, s, True)
            finish_blocks(nc, dve, chain, m, s, True)
        with dve.Else():
            chain.base = before
            finish_blocks(nc, dve, chain, m, s, False)


def index_edges(nc, dve, chain, m, s, wide):
    v = nc.vector
    t0 = T if wide else 0
    values = m.values_wide if wide else m.values
    with dve.Fori(0, G) as g:
        chain.enter(g, 8)
        v.tensor_scalar(m.hi_cols, m.hi[:, bass.ds(g * U, U), :], 1.0, None, op0=ALU.mult).then_inc(s.cols_own, 1)
        v.tensor_scalar(m.lo_cols, m.lo[:, bass.ds(g * U, U), :], 1.0, None, op0=ALU.mult).then_inc(s.cols_own, 1)
        v.tensor_scalar(m.attr_cols, m.attr[:, bass.ds(g * U, U), :], 1.0, None, op0=ALU.mult).then_inc(s.cols_own, 1)
        v.tensor_scalar(m.key_cols, m.key[:, bass.ds(g * U, U), :], 1.0, None, op0=ALU.mult).then_inc(s.cols, 1)
        hold(dve, s.cols, g + (t0 // U + 1), s.ticks_dve)
        hold(dve, s.cols_own, g * 3 + (3 * t0 // U + 3), s.ticks_dve)

        def cells(q):
            hold(dve, s.joined, g * U + (t0 + 2 * q + 2), s.ticks_dve)
            if not wide:
                hold(dve, s.hist, g * 2 + (q + 1), s.ticks_dve)
            v.tensor_tensor(m.cell[:, q, :, :, 0:P],
                            m.iota[:, :].unsqueeze(1).unsqueeze(1).broadcast_to([P, 2, 2, P]),
                            m.lo_cols[:, 2 * q:2 * q + 2, :].unsqueeze(3).broadcast_to([P, 2, 2, P]),
                            op=ALU.is_equal).then_inc(s.cell, 1)
            if not wide:
                v.tensor_tensor(m.node_hi[:, q, :, :, :],
                                m.iota[:, 0:B].unsqueeze(1).unsqueeze(1).broadcast_to([P, 2, 2, B]),
                                m.hi_cols[:, 2 * q:2 * q + 2, :].unsqueeze(3).broadcast_to([P, 2, 2, B]),
                                op=ALU.is_equal).then_inc(s.blocks, 1)

        def weigh(q):
            hold(dve, s.blocks, g * 2 + (q + 1), s.ticks_dve)
            v.tensor_tensor(m.weighted[:, q, :, :, :],
                            m.attr_cols[:, 2 * q:2 * q + 2, :].unsqueeze(2).broadcast_to([P, 2, B, EDGE_DIM]),
                            m.node_hi[:, q, :, 0, :].unsqueeze(3).broadcast_to([P, 2, B, EDGE_DIM]),
                            op=ALU.mult).then_inc(s.hist_in, 1)

        def compare(q):
            hold(dve, s.key_row, g * U + (t0 + 2 * q + 2), s.ticks_dve)
            for tile in range(2):
                v.tensor_tensor(m.same[:, q, tile, :, :], m.key_row[q],
                                m.key_cols[:, 2 * q + tile, :].unsqueeze(2).broadcast_to([P, 2, 2 * P]),
                                op=ALU.is_equal).then_inc(s.same, 1)

        def index(q):
            pair = slice(2 * q, 2 * q + 2)
            hold(dve, s.valued, g * U + (t0 + 2 * q + 4), s.ticks_dve)
            chain.link(v.tensor_tensor(m.late[:, :, :, :], values[:, pair, :, P:ROW], m.limit[:, :, :, :],
                                       op=ALU.is_gt))
            chain.link(v.tensor_tensor(m.spare_late[:, :, :, :], m.late[:, :, :, :],
                                       m.spare[:, :, :].rearrange("p t (w c) -> p t w c", w=2), op=ALU.mult))
            chain.link(v.tensor_tensor(m.late_row[:, :, :], m.spare_late[:, :, :, 0], m.spare_late[:, :, :, 1],
                                       op=ALU.max))
            chain.link(v.tensor_tensor(m.index[:, 4 * q:4 * q + 4].rearrange("p (j w) -> p j w", w=2),
                                       m.late_row[:, :, :], m.key_cols[:, pair, :], op=ALU.max))
            dve.sem_inc(s.indexed, 1)

        cells(0)
        if not wide:
            weigh(0)
        compare(0)
        cells(1)
        compare(1)
        index(0)
        if not wide:
            weigh(1)
        index(1)
    chain.leave(G)


def finish_blocks(nc, dve, chain, m, s, wide):
    passes, last = plan(wide)

    def finish(done, i, p):
        step, b0, n, posts = done
        normed = NORMED_BEFORE.get(step["post"], 0)
        hold(dve, s.product_ready, i * n + (posts + p + 2), s.ticks_dve)
        finish_block(nc, dve, chain, m, s, step, i * n + (b0 + p), i * n + (b0 + p + normed))

    for g, ps in enumerate(passes):
        done, width = ps["done"], ps["n"] * K * P
        n = done[2] if done else 0
        if not (wide and done is None):
            with dve.Fori(0, K) as i:
                chain.enter(i, post_links(done[0]) * n if done else 0)
                for j in range(K):
                    if not wide:
                        cast(dve, m, s, ps, g, i, j, width, True, s.ticks_dve)
                    if done and j in finish_at(n):
                        finish(done, i, finish_at(n).index(j))
            chain.leave(K)
        dve.wait_ge(s.used, K + ps["used"] + B)
        for c, (at, size) in enumerate(cuts(width)):
            if c % 2:
                nc.vector.tensor_copy(m.sums_t[:, at:at + size], m.acc[:, at:at + size]).then_inc(s.evac_dve, 1)
    with dve.Fori(0, K) as i:
        chain.enter(i, post_links(last[0]) * last[2])
        for p in range(last[2]):
            finish(last, i, p)
    chain.leave(K)


def finish_block(nc, dve, chain, m, s, step, b, normed):
    v = nc.vector
    post = step["post"]
    x = one(m.x, b)
    part = [m.product[:, D * n:D * (n + 1)] for n in range(3)]

    def by(name):
        return m.scale[name][:, bass.ds(b, 1)]

    def read():
        dve.sem_inc(s.product_read, 1)

    if post == "add_scaled":
        chain.link(v.scalar_tensor_tensor(x, part[0], by("half_inv_dst"), x, op0=ALU.mult, op1=ALU.add))
        read()
    elif post in ("layer0_end", "layer1_end", "layer2_end"):
        own, following = {"layer0_end": ("half_inv_src", "dis_dst"), "layer1_end": ("dis_dst", "dis_src"),
                          "layer2_end": ("dis_src", None)}[post]
        chain.link(v.scalar_tensor_tensor(m.xn[:, :], part[0], by(own), x, op0=ALU.mult, op1=ALU.add))
        read()
        if post == "layer1_end":
            chain.link(v.tensor_tensor(m.xn[:, :], m.xn[:, :], m.bias1[:, 1, :], op=ALU.add))
        chain.link(v.tensor_scalar(x, m.xn[:, :], 1.0, None, op0=ALU.mult))
        normalize(nc, dve, chain, m, s, normed, by(following) if following else None)
    elif post == "gcn_hidden":
        chain.link(v.scalar_tensor_tensor(m.r[:, :], part[0], by("dis_dst"), m.bias1[:, 0, :],
                                          op0=ALU.mult, op1=ALU.add))
        read()
        chain.link(v.tensor_scalar(m.v[:, :], m.r[:, :], 0.0, by("dis_dst"), op0=ALU.max, op1=ALU.mult))
    elif post == "hop":
        chain.link(v.tensor_scalar(m.v[:, :], part[0], by("dis2_src"), None, op0=ALU.mult))
        read()
    elif post == "edge0":
        chain.link(v.tensor_scalar(m.v[:, :], part[0], by("inv_dst"), None, op0=ALU.mult))
        read()
    elif post == "edge1":
        chain.link(v.tensor_scalar(m.v[:, :], part[0], by("inv_dst"), None, op0=ALU.mult))
        chain.link(v.tensor_scalar(one(m.carry, b), part[1], 1.0, None, op0=ALU.mult))
        chain.link(v.scalar_tensor_tensor(x, part[2], by("inv_dst"), x, op0=ALU.mult, op1=ALU.add))
        read()
    elif post == "edge2":
        chain.link(v.tensor_tensor(m.r[:, :], part[0], one(m.carry, b), op=ALU.add))
        chain.link(v.scalar_tensor_tensor(x, part[1], by("inv_dst"), x, op0=ALU.mult, op1=ALU.add))
        read()
        chain.link(v.tensor_scalar(m.v[:, :], m.r[:, :], by("inv_dst"), None, op0=ALU.mult))
    elif post == "edge3":
        chain.link(v.scalar_tensor_tensor(x, part[0], by("inv_dst"), x, op0=ALU.mult, op1=ALU.add))
        read()
        dve.sem_inc(s.final, 1)
    if step["xout"] is not None:
        write_table(nc, dve, chain, m, s, step["xout"], b)


def tensor_program(nc, block, a, m, s):
    @block.tensor
    def _(pe):
        mm = nc.tensor.matmul
        pe.wait_ge(s.consts, 12)
        pe.wait_ge(s.weights_in, 25 * 16)
        with pe.Fori(0, B) as b:
            hold(pe, s.pre_v, b + 1, s.ticks_pe)
            mm(m.product[:, 0:P], m.v[:, :], m.ident[:, :], start=True, stop=True).then_inc(s.pre_t, 1)
            hold(pe, s.pre_vt, b + 1, s.ticks_pe)
            mm(m.product[:, 0:D], m.vt[:, :], m.w_self[:, :], start=True, stop=False)
            mm(m.product[:, 0:D], m.ones[0:1, :], m.bias0_sum[:, :], start=False, stop=True).then_inc(s.pre_done, 1)

        for bank in m.hist_banks:
            empty(mm, m, bank)
        pe.sem_inc(s.joined, 4)
        pe.sem_inc(s.hist, 2)
        join_edges(nc, pe, m, s, False)
        pe.wait_ge(s.most, 1)
        mm(m.product[0:1, 0:P], m.most[:, 2:3], m.ident[:, :], start=True, stop=True).then_inc(s.most_row, 1)
        with pe.Fori(0, B) as b:
            hold(pe, s.edge_blk, b + 1, s.ticks_pe)
            mm(m.edge_row[0:EC, 0:P], m.edge_block[:, :], m.ident[:, :], start=True, stop=True).then_inc(s.edge_t, 1)

        pe.sem_inc(s.used, K)
        pe.sem_inc(s.cast_act, K)
        pe.sem_inc(s.cast_dve, K)
        pe.sem_inc(s.product_ready, 1)
        pe.sem_inc(s.product_read, 1)
        pe.wait_ge(s.flag_ready, 1)
        wide = pe.value_load(m.flag[0:1, 0:1])
        with pe.If(wide == 1):
            join_edges(nc, pe, m, s, True)
            multiply(nc, pe, m, s, True)
        with pe.Else():
            multiply(nc, pe, m, s, False)


def empty(mm, m, bank):
    mm(bank[:, 0:2], m.nought[:, :], m.nought[:, 0:2], start=True, stop=True, skip_group_check=True)


def join_edges(nc, pe, m, s, wide):
    mm = nc.tensor.matmul
    t0 = T if wide else 0
    with pe.Fori(0, T // U) as g:
        for j in range(U):
            hold(pe, s.diag, g * U + (t0 + j + 1), s.ticks_pe)
            mm(m.key_row[j // 2][:, :, (j % 2) * P:(j % 2 + 1) * P], m.ones[:, :], m.diag[:, j % 2, :, :],
               start=True, stop=True).then_inc(s.key_row, 1)
        for q in range(2):
            hold(pe, s.cell, g * 2 + (t0 // 2 + q + 1), s.ticks_pe)
            hold(pe, s.same, g * U + (t0 + 2 * q + 2), s.ticks_pe)
            for tile in range(2):
                hold(pe, s.valued, g * U + (t0 + 2 * q + tile + 1), s.ticks_pe)
                for w in range(2):
                    for of in range(2):
                        last = mm(m.joined[tile][:, w, :], m.same[:, q, of, w, tile * P:(tile + 1) * P],
                                  m.cell[:, q, of, w, :], start=(of == 0), stop=(of == 1))
                last.then_inc(s.joined, 1)
            if not wide:
                hold(pe, s.lo, g * 2 + (q + 1), s.ticks_pe)
                hold(pe, s.hist_in, g * 2 + (q + 1), s.ticks_pe)
                half = (B - B // 2) * EDGE_DIM
                for tile in range(2):
                    for w in range(2):
                        mm(m.edges_of[w], m.cell[:, q, tile, w, 0:P], m.node_hi[:, q, tile, w, :], start=False,
                           stop=True, skip_group_check=True)
                    flat = m.weighted[:, q, tile, :, :].rearrange("p b c -> p (b c)")
                    mm(m.hist_dst[0], m.node_lo[:, q, tile, :], flat[:, 0:half], start=False, stop=True,
                       skip_group_check=True)
                    last = mm(m.hist_dst[1], m.node_lo[:, q, tile, :], flat[:, half:B * EDGE_DIM], start=False,
                              stop=True, skip_group_check=True)
                last.then_inc(s.hist, 1)


def multiply(nc, pe, m, s, wide):
    mm = nc.tensor.matmul
    passes, last = plan(wide)
    evacuated = [0, 0]

    def product(done, i, p):
        step, _, n, posts = done
        index = i * n + (posts + p)
        wide_w = len(step["w"]) * D
        if step["w"] == ("ident",):
            w = m.ident[:, :]
        else:
            first = m.w_at[step["w"][0]]
            w = m.w[:, first:first + len(step["w"]), :].rearrange("p n d -> p (n d)")
        hold(pe, s.slot_ready, index + 1, s.ticks_pe)
        hold(pe, s.product_read, index + 1, s.ticks_pe)
        edge = step.get("edge")
        done_ = mm(m.product[:, 0:wide_w], m.sums_slot[:, :], w, start=True, stop=edge is None)
        if edge:
            fed = posts - EDGE_POSTS_BEFORE
            hold(pe, s.edge_ready, i * (16 * n) + 16 * (fed + p + 1), s.ticks_pe)
            done_ = mm(m.product[:, 0:D], m.edge_slot[:, :], m.w_edge[:, int(edge[1]), :], start=False, stop=True)
        done_.then_inc(s.product_ready, 1)

    for g, ps in enumerate(passes):
        step, done, width = ps["step"], ps["done"], ps["n"] * K * P
        pieces = cuts(width)
        for c, (at, size) in enumerate(pieces):
            if g and c < len(cuts(passes[g - 1]["n"] * K * P)):
                evacuated[c % 2] += 1
                pe.wait_ge(s.evac_dve if c % 2 else s.evac_act, evacuated[c % 2])
            empty(mm, m, m.acc[:, at:at + size])
        for c in range(len(pieces), len(cuts(passes[g - 1]["n"] * K * P)) if g else 0):
            evacuated[c % 2] += 1

        def halves(i, j, staged):
            hold(pe, s.staged, i * K + (staged + j + 1), s.ticks_pe)
            if wide:
                return [m.staged_wide[:, j % RING, :]]
            return [m.staged_r[:, j % RING, half, :] for half in range(2)]

        if step["loop"]:
            with pe.Fori(0, ps["n"]) as i:
                for j in range(K):
                    for part in halves(i, j, ps["used"] - ps["n"] * K):
                        last_mm = mm(m.acc[:, bass.ds(i * (K * P) + j * P, P)], part,
                                     m.ident[:, :] if wide else m.ident_r[:, :], start=False, stop=True,
                                     skip_group_check=True)
                    last_mm.then_inc(s.used, 1)
        with pe.Fori(0, K) as i:
            for j in range(K):
                if wide:
                    hold(pe, s.rows_in[j % RING], rows_count(g, i, j), s.ticks_pe)
                    rows = m.ring_wide
                else:
                    hold(pe, s.cast_act, i * K + (g * B + K + j + 1), s.ticks_pe)
                    hold(pe, s.cast_dve, i * K + (g * B + K + j + 1), s.ticks_pe)
                    rows = m.rows_r
                for part in halves(i, j, ps["used"]):
                    for at, size in pieces:
                        last_mm = mm(m.acc[:, at:at + size], part, rows[:, j % RING, at:at + size], start=False,
                                     stop=True, skip_group_check=True)
                last_mm.then_inc(s.used, 1)
                if done and j in product_at(done[2]):
                    product(done, i, product_at(done[2]).index(j))
    with pe.Fori(0, K) as i:
        for p in range(last[2]):
            product(last, i, p)


EDGE_POSTS_BEFORE = B * next(n for n, step in enumerate(STEPS) if "edge" in step)


_INS = ["x", "src", "dst", "edge_attr_16", "L0_gnn_W_self", "L0_gnn_b_self", "L0_gnn_W_s2d", "L0_gnn_b_s2d",
        "L0_gnn_W_d2s", "L0_gnn_b_d2s", "L1_gnn_W1", "L1_gnn_b1", "L1_gnn_W2", "L1_gnn_b2", "L3_gnn_W0",
        "L3_gnn_b0", "L3_gnn_W1", "L3_gnn_b1", "L3_gnn_W2", "L3_gnn_b2", "L3_gnn_W3", "L3_gnn_b3"]


def arguments(t):
    w1, w2, w3 = t["L3_gnn_W1"], t["L3_gnn_W2"], t["L3_gnn_W3"]
    a = Names()
    a.x, a.src, a.dst, a.edge_attr, a.out = t["x"], t["src"], t["dst"], t["edge_attr_16"], t["out"]
    a.w_self = t["L0_gnn_W_self"]
    a.w = dict(s2d=t["L0_gnn_W_s2d"], d2s=t["L0_gnn_W_d2s"], g1=t["L1_gnn_W1"], g2=t["L1_gnn_W2"],
               e0=t["L3_gnn_W0"][0:D, :], e1=w1[0:D, :], e2a=w2[0:D, :], e2b=w2[D:2 * D, :],
               e3a=w3[0:D, :], e3b=w3[D:2 * D, :], e3c=w3[2 * D:3 * D, :])
    a.w_edge = [t["L3_gnn_W0"][D:D + EDGE_DIM, :], w1[D:D + EDGE_DIM, :], w2[2 * D:2 * D + EDGE_DIM, :],
                w3[3 * D:3 * D + EDGE_DIM, :]]
    a.b_edge = [t[f"L3_gnn_b{n}"] for n in range(4)]
    a.bias0 = [t["L0_gnn_b_self"], t["L0_gnn_b_s2d"], t["L0_gnn_b_d2s"]]
    a.bias1 = [t["L1_gnn_b1"], t["L1_gnn_b2"]]
    return a


def kernel(**inputs):
    import concourse.bacc as _bacc
    from concourse.bass_utils import run_bass_kernel_spmd as _run

    nc = _bacc.Bacc("TRN2", target_bir_lowering=False, num_devices=1)
    arrays, t = {}, {}
    for name in _INS:
        array = np.ascontiguousarray(inputs[name])
        arrays[f"in_{name}_dram"] = array
        t[name] = nc.dram_tensor(f"in_{name}_dram", array.shape, mybir.dt.from_np(array.dtype),
                                 kind="ExternalInput").ap()
    t["out"] = nc.dram_tensor("out_0_dram", (N, D), F32, kind="ExternalOutput").ap()
    build_gnn(nc, arguments(t))
    r = _run(nc, [arrays], core_ids=[0])
    return r.results[0]["out_0_dram"]
```

```python
from contextlib import ExitStack

import numpy as np
import concourse.bass as bass
from concourse import mybir

N = 6250
E = 106250
D = 128
EDGE_DIM = 16
EC = EDGE_DIM + 1
EPS = 1e-5

P = 128
B = -(-N // P)
NP = B * P
LAST = N - (B - 1) * P
T = 832
FULL = E // T
REST = E - FULL * T
U = 4
G = T // U
ROW = P + 2
K = 7
AHEAD = 2
SCALAR_SHARE = 0.57
BANKS = 7
RING = 4
PAD = NP
ROWS = (B + 1) * P * B
SPARE = (NP + 1) * B + 1
EXACT = 256

F32 = mybir.dt.float32
F32R = mybir.dt.float32r
BF16 = mybir.dt.bfloat16
I32 = mybir.dt.int32
U32 = mybir.dt.uint32
ALU = mybir.AluOpType
ACT = mybir.ActivationFunctionType
AX = mybir.AxisListType.X

STEPS = [
    dict(into="dst", loop=False, w=("s2d",), post="add_scaled", xin=0, xout=None),
    dict(into="src", loop=False, w=("d2s",), post="layer0_end", xin=0, xout=1),
    dict(into="dst", loop=True, w=("g1",), post="gcn_hidden", xin=1, xout=0),
    dict(into="dst", loop=True, w=("g2",), post="layer1_end", xin=0, xout=1),
    dict(into="src", loop=True, w=("ident",), post="hop", xin=1, xout=0),
    dict(into="src", loop=True, w=("ident",), post="hop", xin=0, xout=1),
    dict(into="src", loop=True, w=("ident",), post="layer2_end", xin=1, xout=0),
    dict(into="dst", loop=False, w=("e0",), edge="e0", post="edge0", xin=0, xout=1),
    dict(into="dst", loop=False, w=("e1", "e2a", "e3a"), edge="e1", post="edge1", xin=1, xout=0),
    dict(into="dst", loop=False, w=("e2b", "e3b"), edge="e2", post="edge2", xin=0, xout=1),
    dict(into="dst", loop=False, w=("e3c",), edge="e3", post="edge3", xin=1, xout=None),
]
NORM_LINKS = 5
POST_LINKS = dict(add_scaled=1, layer0_end=2 + NORM_LINKS, gcn_hidden=2, layer1_end=3 + NORM_LINKS, hop=1,
                  layer2_end=2 + NORM_LINKS, edge0=1, edge1=3, edge2=3, edge3=1)


NORMED_BEFORE = {"layer0_end": B, "layer1_end": 2 * B, "layer2_end": 3 * B}


def post_links(step):
    return POST_LINKS[step["post"]] + (1 if step["xout"] is not None else 0)


def back(j):
    return min(d for d in range(1, K + 1) if (j - d) % K % RING == j % RING)


def plan(wide):
    widths = [1] * K if wide else [2, 2, 2, 1]
    passes, posts, done, generation, used, bank = [], 0, None, 0, 0, 0
    for step in STEPS:
        b0 = 0
        for q, n in enumerate(widths):
            pieces = [((bank + c) % BANKS, at, size) for c, (at, size) in enumerate(cuts(K * n * P))]
            bank += len(pieces)
            passes.append(dict(step=step, b0=b0, n=n, done=done, generation=generation, used=used, pieces=pieces))
            used += B
            if done is not None:
                posts += K * done[2]
            done = (step, b0, n, posts)
            b0 += K * n
        if step["xout"] is not None:
            generation += 1
    return passes, done


def rows_count(g, i, j):
    return i * 16 + 16 * (K * g + j // K + 1)


def ring_place(ps, j):
    if ps["n"] == 2:
        return j % RING, 0
    return (j // 2 + RING - 1) % RING, j % 2 * K * P


def ring_back(ps, j):
    if ps["n"] == 2:
        return back(j)
    return min(K, j + K - (K - RING + (j // 2)))


def split(width):
    return 128 * round(width * SCALAR_SHARE / 128)


def cuts(width):
    return [(c, min(512, width - c)) for c in range(0, width, 512)]


class Names:
    pass


def build_gnn(nc, a):
    ctx = ExitStack()
    with ctx:
        def sb(name, shape, dt=F32):
            return ctx.enter_context(nc.sbuf_tensor(name, shape, dt))

        def sem(name):
            return ctx.enter_context(nc.semaphore(name))

        m = Names()
        m.wide_of, m.narrow_of = {}, {}
        for into in ("dst", "src"):
            w = nc.dram_tensor(f"counts_into_{into}", (ROWS, P), F32, kind="Internal").ap()
            m.wide_of[into] = w
            m.narrow_of[into] = w.bitcast(BF16).rearrange("r (h c) -> (r h) c", h=2)[0:ROWS, :]
        m.edge_sums_dram = nc.dram_tensor("edge_sums_t", (EC, NP), F32, kind="Internal").ap()

        m.x = sb("x", [P, B, D])
        table0 = sb("table0", [P, B * D])
        arena = sb("arena", [P, T * EDGE_DIM + 6 * T + NP // 4])
        cut = [0]

        def part(n):
            cut[0] += n
            assert cut[0] <= arena.shape[1]
            return arena[:, cut[0] - n:cut[0]]

        table1 = part(B * D)
        m.table = [t.rearrange("p (b d) -> p b d", b=B) for t in (table0[:, :], table1)]
        m.carry = part(B * D).rearrange("p (b d) -> p b d", b=B)
        ring = part(RING * K * P)
        m.ring_narrow = ring.bitcast(BF16).rearrange("p (j n) -> p j n", j=RING)
        m.ring_wide = ring.rearrange("p (j n) -> p j n", j=RING)
        m.sums_t = part(2 * K * P)
        m.staged_wide = part(RING * D).rearrange("p (j d) -> p j d", j=RING)
        m.edge_sums_t = table1[0:EC, 0:NP]
        cut[0] = 0
        m.attr = part(T * EDGE_DIM).rearrange("p (t c) -> p t c", c=EDGE_DIM)
        m.key = part(2 * T).rearrange("p (t w) -> p t w", w=2)
        m.lo = part(T).bitcast(BF16).rearrange("p (t w) -> p t w", w=2)
        m.hi = part(T).bitcast(BF16).rearrange("p (t w) -> p t w", w=2)
        m.zeros = part(NP // 4)
        raw = part(2 * T)
        m.raw = raw.bitcast(I32).rearrange("p (w t) -> p w t", w=2)
        cut[0] -= 2 * T
        values = part(2 * U * ROW)
        m.values_wide = values.rearrange("p (j w c) -> p j w c", j=U, w=2)
        m.values = values[:, 0:U * ROW].bitcast(BF16).rearrange("p (j w c) -> p j w c", j=U, w=2)
        m.rows_r = sb("rows_r", [P, RING, 2 * K * P], F32R)
        m.staged_r = sb("staged_r", [P, RING, 2, D], F32R)
        m.ident_r = sb("ident_r", [P, P], F32R)
        m.index = sb("index", [P, 2 * U], U32)
        m.diag = sb("diag", [P, 2, 2, P])
        m.same = sb("same", [P, 2, 2, 2, 2 * P], BF16)
        m.cell = sb("cell", [P, 2, 2, 2, ROW], BF16)
        m.mark = sb("mark", [P, 2], I32)
        m.limit = sb("limit", [P, 2, 2, 2])
        m.late = sb("late", [P, 2, 2, 2])
        m.spare_late = sb("spare_late", [P, 2, 2, 2])
        m.late_row = sb("late_row", [P, 2, 2])
        m.node_lo = sb("node_lo", [P, 2, 2, P])
        m.node_hi = sb("node_hi", [P, 2, 2, 2, B], BF16)
        m.weighted = sb("weighted", [P, 2, 2, B, EDGE_DIM])
        m.edge_blocks = m.weighted[:, :, :, :, :].rearrange("p q t b c -> p (q t b c)")[:, 0:K * EC].rearrange(
            "p (b c) -> p b c", c=EC)

        m.ident = sb("ident", [P, P])
        m.ones = sb("ones", [P, P])
        m.iota = sb("iota", [P, P])
        m.iota_i = sb("iota_i", [P, P], I32)
        m.spare_i = sb("spare_i", [P, 2], I32)
        m.spare = sb("spare", [P, 2, 4])
        m.nought = sb("nought", [P, P], BF16)

        m.w_self = sb("w_self", [P, D])
        m.w = sb("w", [P, 11, D])
        names = ("s2d", "d2s", "g1", "g2", "e0", "e1", "e2a", "e3a", "e2b", "e3b", "e3c")
        m.w_at = {name: n for n, name in enumerate(names)}
        m.w_edge = sb("w_edge", [EC, 4, D])
        m.bias0 = sb("bias0", [1, 3, D])
        m.bias0_sum = sb("bias0_sum", [1, D])
        m.bias1 = sb("bias1", [P, 2, D])

        m.edge_sums = sb("edge_sums", [P, B, EC])
        m.n_src = sb("n_src", [P, B])
        m.scale = {k: sb(k, [P, B]) for k in ("inv_dst", "inv_src", "half_inv_dst", "half_inv_src",
                                              "dis_dst", "dis_src", "dis2_src")}
        m.most = sb("most", [P, 3])
        m.flag = sb("flag", [1, 4], I32)

        m.sums_slot = sb("sums_slot", [P, P])
        m.edge_slot = sb("edge_slot", [EC, P])
        m.xn = sb("xn", [P, D])
        m.stats = sb("stats", [P, 6])
        m.meanvar = sb("meanvar", [P, 2])
        m.std = sb("std", [P, 1])
        m.rstd = sb("rstd", [P, 1])
        m.eps = sb("eps", [P, 1])
        m.nil = sb("nil", [P, 1])
        m.root = {end: sb(f"root_{end}", [P, B]) for end in ("dst", "src")}
        m.v = sb("v", [P, D])
        m.r = sb("r", [P, D])
        m.vt = sb("vt", [P, D])

        psum = ctx.enter_context(nc.psum_tensor("psum", [P, 8, 512], F32))
        m.acc = [psum[:, bank, :] for bank in range(BANKS)]
        m.product = psum[:, BANKS, :]
        m.hist_dst = [psum[:, 0, 0:(B - B // 2) * EDGE_DIM], psum[:, 1, 0:(B // 2) * EDGE_DIM]]
        m.hist_banks = [psum[:, 0, :], psum[:, 1, :]]
        m.edges_of = [psum[:, 1, 512 - 2 * B:512 - B], psum[:, 1, 512 - B:512]]
        m.joined = [psum[:, 2 + j, 0:2 * ROW].rearrange("p (w c) -> p w c", w=2) for j in range(2)]
        m.key_row = [psum[:, 4 + q, :].rearrange("p (w c) -> p w c", w=2) for q in range(2)]
        m.edge_row = [psum[:, 6, :], psum[:, 7, :]]

        s = Names()
        s.edges_in = sem("edges_in")
        s.blocks = sem("blocks")
        s.lo = sem("lo")
        s.cell = sem("cell")
        s.most = sem("most")
        s.most_row = sem("most_row")
        s.zeroed = sem("zeroed")
        s.landed = sem("landed")
        s.var = sem("var")
        s.std = sem("std")
        s.degree = sem("degree")
        s.root = sem("root")
        s.attr_in = sem("attr_in")
        s.x_in = sem("x_in")
        s.weights_in = sem("weights_in")
        s.consts = sem("consts")
        s.pads = sem("pads")
        s.zeros_set = sem("zeros_set")
        s.diag = sem("diag")
        s.key_row = sem("key_row")
        s.same = sem("same")
        s.indexed = sem("indexed")
        s.joined = sem("joined")
        s.valued = sem("valued")
        s.hist_in = sem("hist_in")
        s.hist = sem("hist")
        s.flag_ready = sem("flag_ready")
        s.chain = sem("chain")
        s.pre_v = sem("pre_v")
        s.pre_t = sem("pre_t")
        s.pre_vt = sem("pre_vt")
        s.pre_done = sem("pre_done")
        s.edge_blk = sem("edge_blk")
        s.edge_t = sem("edge_t")
        s.edge_out = sem("edge_out")
        s.edge_stored = sem("edge_stored")
        s.into_dst = sem("into_dst")
        s.into_src = sem("into_src")
        s.wide_dst = sem("wide_dst")
        s.wide_src = sem("wide_src")
        s.used = sem("used")
        s.cast_act = sem("cast_act")
        s.cast_dve = sem("cast_dve")
        s.evac_act = sem("evac_act")
        s.evac_dve = sem("evac_dve")
        s.halved = sem("halved")
        s.table_ready = sem("table_ready")
        s.slot_ready = sem("slot_ready")
        s.edge_ready = sem("edge_ready")
        s.product_ready = sem("product_ready")
        s.product_read = sem("product_read")
        s.low = sem("low")
        s.staged = sem("staged")
        s.final = sem("final")
        s.out_stored = sem("out_stored")
        s.ticks_pe = sem("ticks_pe")
        s.ticks_act = sem("ticks_act")
        s.ticks_dve = sem("ticks_dve")
        s.ticks_pool = sem("ticks_pool")
        s.rows_in = [sem(f"rows_in_{j}") for j in range(K)]
        s.spare_narrow, s.spare_wide = 2 * 16, 4 * 16

        block = ctx.enter_context(nc.Block())
        sync_program(nc, block, a, m, s)
        pool_program(nc, block, a, m, s)
        scalar_program(nc, block, a, m, s)
        vector_program(nc, block, a, m, s)
        tensor_program(nc, block, a, m, s)


def hold(eng, sem, value, ticks):
    eng.wait_ge(sem, value)
    eng.sem_inc(ticks, 1)


def rows_of(m, into, wide):
    flat = (m.wide_of if wide else m.narrow_of)[into]
    return flat.rearrange("(n b) c -> n (b c)", b=B)


def sync_program(nc, block, a, m, s):
    @block.sync
    def _(sp):
        sp.wait_ge(s.pads, 1)
        for w, ends in ((0, a.dst), (1, a.src)):
            sp.dma_start(m.raw[0:FULL, w, :], ends[0:FULL * T].rearrange("(p t) -> p t", t=T)).then_inc(s.edges_in, 16)
            sp.dma_start(m.raw[FULL:FULL + 1, w, 0:REST],
                         ends[FULL * T:E].rearrange("(p t) -> p t", p=1)).then_inc(s.edges_in, 16)
        sp.wait_ge(s.pads, 2)
        for b in range(0, B - 1, 16):
            sp.dma_start(m.x[:, b:b + 16, :], a.x[b * P:(b + 16) * P, :].rearrange("(b p) d -> p b d", p=P)).then_inc(
                s.x_in, 16)
        sp.dma_start(m.x[0:LAST, B - 1, :], a.x[(B - 1) * P:N, :]).then_inc(s.x_in, 16)
        for w in ("s2d", "d2s", "g1", "g2", "e0", "e1", "e2a", "e3a", "e2b", "e3b", "e3c"):
            sp.dma_start(m.w[:, m.w_at[w], :], a.w[w]).then_inc(s.weights_in, 16)
        sp.dma_start(m.w_self[:, :], a.w_self).then_inc(s.weights_in, 16)
        for n in range(4):
            sp.dma_start(m.w_edge[0:EDGE_DIM, n, :], a.w_edge[n]).then_inc(s.weights_in, 16)
            sp.dma_start(m.w_edge[EDGE_DIM:EC, n, :], a.b_edge[n].rearrange("(o d) -> o d", o=1)).then_inc(
                s.weights_in, 16)
        for n in range(3):
            sp.dma_start(m.bias0[0:1, n, :], a.bias0[n].rearrange("(o d) -> o d", o=1)).then_inc(s.weights_in, 16)
        for n in range(2):
            sp.dma_start(m.bias1[:, n, :], a.bias1[n].rearrange("(o d) -> o d", o=1).broadcast_to([P, D])).then_inc(
                s.weights_in, 16)
        sp.wait_ge(s.pads, 3)
        whole = T * EDGE_DIM
        attr = m.attr.rearrange("p t c -> p (t c)")
        source = a.edge_attr.rearrange("e c -> (e c)")
        for p0, p1 in ((0, 112), (112, FULL)):
            sp.dma_start(attr[p0:p1, :], source[p0 * whole:p1 * whole].rearrange("(p t) -> p t", t=whole)).then_inc(
                s.attr_in, 16)
        sp.dma_start(attr[FULL:FULL + 1, 0:REST * EDGE_DIM],
                     source[FULL * whole:].rearrange("(p t) -> p t", p=1)).then_inc(s.attr_in, 16)
        sp.wait_ge(s.zeros_set, 1)
        fill_zeros(sp, m, s, False)
        sp.wait_ge(s.edge_out, 2 * K + 2)
        sp.dma_start(m.edge_sums_dram, m.edge_sums_t[:, :]).then_inc(s.edge_stored, 16)

        sp.wait_ge(s.flag_ready, 1)
        wide = sp.value_load(m.flag[0:1, 0:1])
        with sp.If(wide == 1):
            sp.wait_ge(s.into_dst, s.spare_narrow + 16 * T)
            sp.wait_ge(s.into_src, s.spare_narrow + 16 * T)
            sp.wait_ge(s.zeros_set, 2)
            fill_zeros(sp, m, s, True)
            stream_rows(sp, a, m, s, True)
        with sp.Else():
            stream_rows(sp, a, m, s, False)
        sp.wait_ge(s.out_stored, 2 * 16)


def fill_zeros(sp, m, s, wide):
    zeros = m.zeros if wide else m.zeros.bitcast(BF16)
    n = zeros.shape[1]
    for into in ("dst", "src"):
        rows = rows_of(m, into, wide)
        with sp.Fori(0, B) as b:
            for c in range(0, NP, n):
                sp.dma_start(rows[bass.ds(b * P, P), c:c + n], zeros).then_inc(s.zeroed, 16)


def stream_rows(sp, a, m, s, wide):
    passes, _ = plan(wide)
    ring = m.ring_wide if wide else m.ring_narrow
    start = (s.spare_wide if wide else s.spare_narrow) + 16 * T
    sp.wait_ge(s.wide_dst if wide else s.into_dst, start)
    sp.wait_ge(s.wide_src if wide else s.into_src, start)
    sp.wait_ge(s.edge_stored, 16)
    for g, ps in enumerate(passes):
        rows = rows_of(m, ps["step"]["into"], wide)
        width = ps["n"] * K * P
        with sp.Fori(0, K) as i:
            for j in range(K):
                free = K - (back(j) if wide else ring_back(ps, j)) + j + 1
                if wide:
                    sp.wait_ge(s.used, i * K + (ps["used"] + free))
                else:
                    sp.wait_ge(s.cast_act, i * K + (g * B + free))
                    sp.wait_ge(s.cast_dve, i * K + (g * B + free))
                slot, at = (j % RING, 0) if wide else ring_place(ps, j)
                sp.dma_start(ring[:, slot, at:at + width],
                             rows[bass.ds(i * (K * P) + j * P, P), ps["b0"] * P:ps["b0"] * P + width]).then_inc(
                                 s.rows_in[j], 16)
    sp.wait_ge(s.final, B)
    sp.dma_start(a.out[0:(B - 1) * P, :].rearrange("(b p) d -> p b d", p=P), m.x[:, 0:B - 1, :]).then_inc(
        s.out_stored, 16)
    sp.dma_start(a.out[(B - 1) * P:N, :], m.x[0:LAST, B - 1, :]).then_inc(s.out_stored, 16)


def pool_program(nc, block, a, m, s):
    @block.gpsimd
    def _(pool):
        pool.memset(m.raw, PAD).then_inc(s.pads, 1)
        pool.memset(m.x[:, B - 1, :], 0.0).then_inc(s.pads, 1)
        pool.memset(m.attr[:, REST:T, :], 0.0).then_inc(s.pads, 1)
        pool.iota(m.iota_i[:, :], pattern=[[1, P]], base=0, channel_multiplier=0).then_inc(s.consts, 1)
        pool.iota(m.spare_i[:, :], pattern=[[P, 2]], base=SPARE, channel_multiplier=1).then_inc(s.consts, 1)
        pool.iota(m.mark[:, 0:1], pattern=[[0, 1]], base=190 << 23, channel_multiplier=-(1 << 23)).then_inc(
            s.consts, 1)
        pool.iota(m.mark[:, 1:2], pattern=[[0, 1]], base=191 << 23, channel_multiplier=-(1 << 23)).then_inc(
            s.consts, 1)
        pool.memset(m.cell[:, :, :, :, P:ROW], 0.0).then_inc(s.consts, 1)
        pool.memset(m.limit[:, :, :, :], 0.0).then_inc(s.consts, 1)
        pool.memset(m.ones[:, :], 1.0).then_inc(s.consts, 1)
        pool.memset(m.nought[:, :], 0.0).then_inc(s.consts, 1)
        pool.memset(m.eps[:, :], EPS).then_inc(s.consts, 1)
        pool.memset(m.nil[:, :], 0.0).then_inc(s.consts, 1)
        pool.wait_ge(s.consts, 10)
        pool.affine_select(out=m.ident[:, :], in_=m.ones[:, :], compare_op=ALU.is_equal, fill=0.0,
                           base=0, pattern=[[-1, P]], channel_multiplier=1).then_inc(s.consts, 1)
        pool.wait_ge(s.consts, 11)
        pool.tensor_copy(m.ident_r[:, :], m.ident[:, :]).then_inc(s.consts, 1)
        pool.sem_inc(s.landed, 2)
        add_edges(pool, m, s, False)

        pool.wait_ge(s.flag_ready, 1)
        wide = pool.value_load(m.flag[0:1, 0:1])
        with pool.If(wide == 1):
            add_edges(pool, m, s, True)
            feed_blocks(pool, m, s, True)
        with pool.Else():
            feed_blocks(pool, m, s, False)


def add_edges(pool, m, s, wide):
    values = m.values_wide if wide else m.values
    done = (s.wide_dst, s.wide_src) if wide else (s.into_dst, s.into_src)
    flat = m.wide_of if wide else m.narrow_of
    before = T if wide else 0
    zeros = m.zeros if wide else m.zeros.bitcast(BF16)
    n = zeros.shape[1]
    spare = 16 * (NP // n)
    pool.wait_ge(s.zeros_set, 2 if wide else 1)
    if wide:
        pool.wait_ge(s.into_dst, s.spare_narrow + 16 * T)
        pool.wait_ge(s.into_src, s.spare_narrow + 16 * T)
    for w, into in enumerate(("dst", "src")):
        for c in range(0, NP, n):
            pool.dma_start(rows_of(m, into, wide)[B * P:(B + 1) * P, c:c + n], zeros).then_inc(done[w], 16)
    pool.wait_ge(s.zeroed, 2 * B * (s.spare_narrow + (s.spare_wide if wide else 0)))
    with pool.Fori(0, G) as g:
        for q in range(2):
            hold(pool, s.valued, g * U + (before + 2 * q + 4), s.ticks_pool)
            hold(pool, s.indexed, g * 2 + (before // 2 + q + 1), s.ticks_pool)
            for w, into in enumerate(("dst", "src")):
                hold(pool, done[w], g * (16 * U) + (spare + 32 * q), s.ticks_pool)
                if into == "src":
                    pool.sem_inc(s.landed, 1)
                for j in (2 * q, 2 * q + 1):
                    pool.indirect_dma_start(
                        out=flat[into], out_offset=bass.IndirectOffsetOnAxis(ap=m.index[:, 2 * j + w:2 * j + w + 1], axis=0),
                        in_=values[:, j, w, 0:P], in_offset=None, compute_op=ALU.add).then_inc(done[w], 16)


def feed_blocks(pool, m, s, wide):
    passes, last = plan(wide)

    def feed(done, i, p):
        _, b0, n, posts = done
        hold(pool, s.product_ready, i * n + (posts + p + 1), s.ticks_pool)
        pool.dma_start(m.edge_slot[:, :], m.edge_sums_dram[:, bass.ds(i * (n * P) + (b0 + p) * P, P)]).then_inc(
            s.edge_ready, 16)

    def stage(ps, i, j):
        slot, used = j % RING, ps["used"]
        block = one(m.table[ps["step"]["xin"]], i * K + j)
        if wide:
            block_waits(pool, s, ps, i, j, s.ticks_pool)
            pool.tensor_copy(m.staged_wide[:, slot, :], block).then_inc(s.staged, 1)
        else:
            hold(pool, s.halved, i * K + (used + j + 1), s.ticks_pool)
            pool.tensor_tensor(m.staged_r[:, slot, 1, :], block, m.staged_r[:, slot, 0, :].bitcast(F32),
                               op=ALU.subtract).then_inc(s.low, 1)
            hold(pool, s.cast_act, i * K + (used + K + j + 1), s.ticks_pool)
            hold(pool, s.cast_dve, i * K + (used + K + j + 1), s.ticks_pool)
            pool.wait_ge(s.low, i * K + (used + j + 1))
            pool.sem_inc(s.staged, 1)

    pool.wait_ge(s.edge_stored, 16)
    for ps in passes:
        done = ps["done"]
        feeds = done is not None and "edge" in done[0]
        with pool.Fori(0, K) as i:
            for j in range(K):
                if feeds and j in feed_at(done[2]):
                    feed(done, i, feed_at(done[2]).index(j))
                stage(ps, i, j)
    with pool.Fori(0, K) as i:
        for p in range(last[2]):
            feed(last, i, p)


def block_waits(eng, s, ps, i, j, ticks):
    if ps["b0"] == 0:
        hold(eng, s.table_ready, i * K + (ps["generation"] * B + j + 1), ticks)
    hold(eng, s.used, i * K + (ps["used"] + K - back(j % K) + j + 1), ticks)


def product_at(n):
    return [2, 5][0:n]


def slot_at(n):
    return [0, 4][0:n]


def feed_at(n):
    return [0, 4][0:n]


def finish_at(n):
    return [3, 6][0:n]


def scalar_program(nc, block, a, m, s):
    @block.scalar
    def _(act):
        act.wait_ge(s.consts, 12)
        act.sem_inc(s.valued, 2)
        with act.Fori(0, B) as b:
            deviation(nc, act, m, s, b)
            hold(act, s.pre_t, b + 1, s.ticks_act)
            nc.scalar.copy(m.vt[:, :], m.product[:, 0:P]).then_inc(s.pre_vt, 1)
        spread_keys(nc, act, m, s, False)
        act.wait_ge(s.degree, 2)
        for end in ("dst", "src"):
            nc.scalar.activation(m.root[end][:, :], m.scale[f"dis_{end}"][:, :], ACT.Sqrt, bias=m.nil[:, :]).then_inc(
                s.root, 1)
        with act.Fori(0, K) as i:
            hold(act, s.edge_t, i + 1, s.ticks_act)
            for j, n in ((0, 4), (4, K - 4)):
                nc.scalar.copy(m.edge_sums_t[:, bass.ds(i * (K * P) + j * P, n * P)],
                               m.edge_row[j // 4][0:EC, 0:n * P]).then_inc(s.edge_out, 1)

        act.wait_ge(s.flag_ready, 1)
        wide = act.value_load(m.flag[0:1, 0:1])
        with act.If(wide == 1):
            act.wait_ge(s.into_dst, s.spare_narrow + 16 * T)
            act.wait_ge(s.into_src, s.spare_narrow + 16 * T)
            spread_keys(nc, act, m, s, True)
            hand_over_sums(nc, act, m, s, True)
        with act.Else():
            hand_over_sums(nc, act, m, s, False)


def deviation(nc, act, m, s, index):
    hold(act, s.var, index + 1, s.ticks_act)
    nc.scalar.activation(m.std[:, :], m.meanvar[:, 1:2], ACT.Sqrt, bias=m.eps[:, :]).then_inc(s.std, 1)


def spread_keys(nc, act, m, s, wide):
    values = m.values_wide if wide else m.values
    t0 = T if wide else 0

    def diagonals(g, q):
        for tile in range(2):
            hold(act, s.key_row, g * U + (t0 + 2 * q + tile + 1), s.ticks_act)
            for w in range(2):
                last = nc.scalar.activation(m.diag[:, tile, w, :], m.ident[:, :], ACT.Copy,
                                            scale=m.key[:, bass.ds(g * U + (2 * q + tile), 1), w])
            last.then_inc(s.diag, 1)

    def take(g, q):
        if not wide:
            hold(act, s.cell, g * 2 + (q + 1), s.ticks_act)
            nc.scalar.copy(m.node_lo[:, q, :, :], m.cell[:, q, :, 0, 0:P]).then_inc(s.lo, 1)
        hold(act, s.landed, g * 2 + (t0 // 2 + q + 2), s.ticks_act)
        for tile in range(2):
            j = 2 * q + tile
            hold(act, s.joined, g * U + (t0 + j + 5), s.ticks_act)
            nc.scalar.copy(values[:, j, :, :], m.joined[tile]).then_inc(s.valued, 1)

    diagonals(0, 0)
    diagonals(0, 1)
    with act.Fori(0, G - 1) as g:
        for q in range(2):
            diagonals(g, q + 2)
            take(g, q)
    take(G - 1, 0)
    take(G - 1, 1)


def hand_over_sums(nc, act, m, s, wide):
    passes, last = plan(wide)
    evacuated = [0, 0]

    def slot(done, i, p):
        _, b0, n, posts = done
        hold(act, s.product_read, i * n + (posts + p + 1), s.ticks_act)
        nc.scalar.copy(m.sums_slot[:, :], m.sums_t[:, bass.ds(i * (n * P) + p * P, P)]).then_inc(s.slot_ready, 1)

    def root(done, i, p):
        step, b0, n, _ = done
        if step["post"] in NORMED_BEFORE:
            deviation(nc, act, m, s, i * n + (b0 + p + NORMED_BEFORE[step["post"]]))

    def cast_block(g, i, j):
        if not wide:
            block_waits(act, s, passes[g], i, j, s.ticks_act)
            nc.scalar.copy(m.staged_r[:, j % K % RING, 0, :],
                           one(m.table[passes[g]["step"]["xin"]], i * K + j)).then_inc(s.halved, 1)
            cast(act, m, s, passes, g, i, j, False, s.ticks_act)

    for g, ps in enumerate(passes):
        done = ps["done"]
        n = done[2] if done else 0
        if g:
            act.wait_ge(s.evac_act, evacuated[0])
            act.wait_ge(s.evac_dve, evacuated[1])

        def beside(i, j):
            if done and j in finish_at(n):
                root(done, i, finish_at(n).index(j))
            if done and j in slot_at(n):
                slot(done, i, slot_at(n).index(j))

        if not (wide and done is None):
            rounds(act, passes, g, cast_block, beside)
        act.wait_ge(s.used, K + ps["used"] + B)
        for c, (bank, at, size) in enumerate(ps["pieces"]):
            if c % 2 == 0:
                nc.scalar.copy(m.sums_t[:, at:at + size], m.acc[bank][:, 0:size]).then_inc(s.evac_act, 1)
            evacuated[c % 2] += 1
    act.wait_ge(s.evac_act, evacuated[0])
    act.wait_ge(s.evac_dve, evacuated[1])
    with act.Fori(0, K) as i:
        for p in range(last[2]):
            slot(last, i, p)
            root(last, i, p)


def rounds(eng, passes, g, cast_block, beside, chain=None, links=0):
    if g == 0:
        for j in range(AHEAD):
            cast_block(g, 0, j)
    with eng.Fori(0, K - 1) as i:
        if chain:
            chain.enter(i, links)
        for j in range(K):
            cast_block(g, i, j + AHEAD)
            beside(i, j)
    if chain:
        chain.leave(K - 1)
    for j in range(K):
        if j + AHEAD < K:
            cast_block(g, K - 1, j + AHEAD)
        elif g + 1 < len(passes):
            cast_block(g + 1, 0, j + AHEAD - K)
        beside(K - 1, j)


def cast(eng, m, s, passes, g, i, j, by_vector, ticks):
    ps = passes[g]
    slot, width = j % K % RING, ps["n"] * K * P
    hold(eng, s.rows_in[j % K], rows_count(g, i, j), ticks)
    if by_vector:
        hold(eng, s.used, i * K + (ps["used"] + K - back(j % K) + j + 1), ticks)
    at = split(width)
    place, start = ring_place(ps, j % K)
    if by_vector:
        eng.tensor_copy(m.rows_r[:, slot, at:width], m.ring_narrow[:, place, start + at:start + width]).then_inc(s.cast_dve, 1)
    else:
        eng.copy(m.rows_r[:, slot, 0:at], m.ring_narrow[:, place, start:start + at]).then_inc(s.cast_act, 1)


class Chain:

    def __init__(self, dve, sem):
        self.dve, self.sem, self.base, self.at, self.turn, self.each = dve, sem, 0, 0, None, 0

    def enter(self, turn, each):
        self.turn, self.each, self.at = turn, each, 0

    def leave(self, rounds):
        assert self.at == self.each, (self.at, self.each)
        self.base += rounds * self.each
        self.turn = None

    def link(self, instruction):
        instruction.then_inc(self.sem, 1)
        if self.turn is None:
            self.base += 1
            self.dve.wait_ge(self.sem, self.base)
        else:
            self.at += 1
            self.dve.wait_ge(self.sem, self.turn * self.each + (self.base + self.at))


def one(tensor, b):
    return tensor[:, bass.ds(b, 1), :].rearrange("p o d -> p (o d)")


def normalize(nc, dve, chain, m, s, index, scale=None):
    v = nc.vector
    chain.link(v.bn_stats(m.stats[:, :], m.xn[:, :]))
    dve.sem_inc(s.ticks_dve, 1)
    chain.link(v.bn_aggr(m.meanvar[:, :], m.stats[:, :]))
    dve.sem_inc(s.var, 1)
    hold(dve, s.std, index + 1, s.ticks_dve)
    chain.link(v.reciprocal(m.rstd[:, :], m.std[:, :]))
    chain.link(v.tensor_scalar(m.r[:, :], m.xn[:, :], m.meanvar[:, 0:1], m.rstd[:, :],
                               op0=ALU.subtract, op1=ALU.mult))
    if scale is None:
        chain.link(v.tensor_scalar(m.v[:, :], m.r[:, :], 0.0, None, op0=ALU.max))
    else:
        chain.link(v.tensor_scalar(m.v[:, :], m.r[:, :], 0.0, scale, op0=ALU.max, op1=ALU.mult))


def write_table(nc, dve, chain, m, s, table, b):
    chain.link(nc.vector.tensor_scalar(one(m.table[table], b), m.v[:, :], 1.0, None, op0=ALU.mult))
    dve.sem_inc(s.table_ready, 1)


def vector_program(nc, block, a, m, s):
    @block.vector
    def _(dve):
        v = nc.vector
        chain = Chain(dve, s.chain)
        dve.wait_ge(s.consts, 12)
        chain.link(v.tensor_copy(m.iota[:, :], m.iota_i[:, :]))
        chain.link(v.tensor_copy(m.spare[:, :, :], m.spare_i[:, :].unsqueeze(2).broadcast_to([P, 2, 4])))
        mark = m.mark[:, :].bitcast(F32)
        for tile in range(2):
            for pair in range(2):
                chain.link(v.tensor_copy(m.cell[:, pair, tile, :, P + tile], mark[:, 0:1].broadcast_to([P, 2])))
            chain.link(v.tensor_copy(m.limit[:, tile, :, tile], mark[:, 1:2].broadcast_to([P, 2])))
        chain.link(v.memset(m.limit[:, 0, :, 1], 3e38))
        dve.wait_ge(s.pads, 3)
        v.memset(m.zeros, 0.0).then_inc(s.zeros_set, 1)

        dve.wait_ge(s.edges_in, 4 * 16)
        whole = m.key.rearrange("p t w -> p (t w)").bitcast(I32).rearrange("p (w t) -> p w t", w=2)
        chain.link(v.tensor_single_scalar(whole, m.raw, P - 1, op=ALU.bitwise_and))
        chain.link(v.tensor_copy(m.lo.rearrange("p t w -> p w t"), whole))
        chain.link(v.tensor_single_scalar(whole, m.raw, 7, op=ALU.logical_shift_right))
        chain.link(v.tensor_copy(m.hi.rearrange("p t w -> p w t"), whole))
        for w in range(2):
            chain.link(v.scalar_tensor_tensor(m.key[:, :, w], m.hi[:, :, 1 - w], float(P), m.lo[:, :, 1 - w],
                                              op0=ALU.mult, op1=ALU.add))
            chain.link(v.scalar_tensor_tensor(m.key[:, :, w], m.key[:, :, w], float(B), m.hi[:, :, w],
                                              op0=ALU.mult, op1=ALU.add))

        dve.wait_ge(s.x_in, 4 * 16)
        dve.wait_ge(s.weights_in, 25 * 16)
        chain.link(v.tensor_tensor(m.bias0_sum[:, :], m.bias0[:, 1, :], m.bias0[:, 2, :], op=ALU.add))
        chain.link(v.scalar_tensor_tensor(m.bias0_sum[:, :], m.bias0_sum[:, :], 0.5, m.bias0[:, 0, :],
                                          op0=ALU.mult, op1=ALU.add))
        with dve.Fori(0, B) as b:
            chain.enter(b, 1 + NORM_LINKS + 1 + 1)
            chain.link(v.tensor_scalar(m.xn[:, :], one(m.x, b), 1.0, None, op0=ALU.mult))
            normalize(nc, dve, chain, m, s, b)
            dve.sem_inc(s.pre_v, 1)
            write_table(nc, dve, chain, m, s, 0, b)
            hold(dve, s.pre_done, b + 1, s.ticks_dve)
            chain.link(v.tensor_tensor(one(m.x, b), m.product[:, 0:D], one(m.x, b), op=ALU.add))
        chain.leave(B)

        dve.wait_ge(s.attr_in, 3 * 16)
        index_edges(nc, dve, chain, m, s, False)

        dve.wait_ge(s.hist, T // 2 + 2)
        half = B - B // 2
        for (b0, b1), sums in zip(((0, half), (half, B)), m.hist_dst):
            chain.link(v.tensor_copy(m.edge_sums[:, b0:b1, 0:EDGE_DIM], sums.rearrange("p (b c) -> p b c", c=EDGE_DIM)))
        chain.link(v.tensor_copy(m.edge_sums[:, :, EDGE_DIM], m.edges_of[0]))
        chain.link(v.tensor_copy(m.n_src[:, :], m.edges_of[1]))
        n_dst = m.edge_sums[:, :, EDGE_DIM]
        for end, n in (("dst", n_dst), ("src", m.n_src[:, :])):
            inv, half_inv = m.scale[f"inv_{end}"][:, :], m.scale[f"half_inv_{end}"][:, :]
            chain.link(v.tensor_scalar(inv, n, 1.0, None, op0=ALU.max))
            chain.link(v.reciprocal(inv, inv))
            chain.link(v.tensor_scalar(half_inv, inv, 0.5, None, op0=ALU.mult))
            chain.link(v.tensor_scalar(m.scale[f"dis_{end}"][:, :], n, 1.0, None, op0=ALU.add))
            dve.sem_inc(s.degree, 1)
        dve.wait_ge(s.root, 2)
        for end in ("dst", "src"):
            chain.link(v.reciprocal(m.scale[f"dis_{end}"][:, :], m.root[end][:, :]))
        chain.link(v.tensor_tensor(m.scale["dis2_src"][:, :], m.scale["dis_src"][:, :], m.scale["dis_src"][:, :],
                                   op=ALU.mult))
        chain.link(v.tensor_reduce(out=m.most[:, 0:1], in_=n_dst, axis=AX, op=ALU.max))
        chain.link(v.tensor_reduce(out=m.most[:, 1:2], in_=m.n_src[:, :], axis=AX, op=ALU.max))
        v.tensor_tensor(m.most[:, 2:3], m.most[:, 0:1], m.most[:, 1:2], op=ALU.max).then_inc(s.most, 1)
        dve.wait_ge(s.most_row, 1)
        chain.link(v.tensor_reduce(out=m.rstd[0:1, 0:1], in_=m.product[0:1, 0:P], axis=AX, op=ALU.max))
        v.tensor_scalar(m.flag[0:1, 0:1], m.rstd[0:1, 0:1], float(EXACT), None, op0=ALU.is_gt).then_inc(
            s.flag_ready, 1)
        with dve.Fori(0, K) as i:
            v.tensor_scalar(m.edge_blocks[:, :, :], m.edge_sums[:, bass.ds(i * K, K), :], 1.0, None,
                            op0=ALU.mult).then_inc(s.edge_blk, 1)
            hold(dve, s.edge_t, i + 1, s.ticks_dve)

        dve.wait_ge(s.flag_ready, 1)
        wide = dve.value_load(m.flag[0:1, 0:1])
        before = chain.base
        with dve.If(wide == 1):
            dve.wait_ge(s.edge_stored, 16)
            v.memset(m.zeros, 0.0).then_inc(s.zeros_set, 1)
            dve.wait_ge(s.into_dst, s.spare_narrow + 16 * T)
            dve.wait_ge(s.into_src, s.spare_narrow + 16 * T)
            index_edges(nc, dve, chain, m, s, True)
            finish_blocks(nc, dve, chain, m, s, True)
        with dve.Else():
            chain.base = before
            finish_blocks(nc, dve, chain, m, s, False)


def index_edges(nc, dve, chain, m, s, wide):
    v = nc.vector
    t0 = T if wide else 0
    values = m.values_wide if wide else m.values

    def cells(g, q):
        hold(dve, s.joined, g * U + (t0 + 2 * q + 2), s.ticks_dve)
        if not wide:
            hold(dve, s.hist, g * 2 + (q + 1), s.ticks_dve)
        tiles = bass.ds(g * U + 2 * q, 2)
        v.tensor_tensor(m.cell[:, q % 2, :, :, 0:P],
                        m.iota[:, :].unsqueeze(1).unsqueeze(1).broadcast_to([P, 2, 2, P]),
                        m.lo[:, tiles, :].unsqueeze(3).broadcast_to([P, 2, 2, P]),
                        op=ALU.is_equal).then_inc(s.cell, 1)
        if not wide:
            v.tensor_tensor(m.node_hi[:, q % 2, :, :, :],
                            m.iota[:, 0:B].unsqueeze(1).unsqueeze(1).broadcast_to([P, 2, 2, B]),
                            m.hi[:, tiles, :].unsqueeze(3).broadcast_to([P, 2, 2, B]),
                            op=ALU.is_equal).then_inc(s.blocks, 1)

    def compare(g, q):
        hold(dve, s.key_row, g * U + (t0 + 2 * q + 4), s.ticks_dve)
        for tile in range(2):
            v.tensor_tensor(m.same[:, q % 2, tile, :, :], m.key_row[q % 2],
                            m.key[:, bass.ds(g * U + (2 * q + tile), 1), :].rearrange("p o w -> p (o w)").unsqueeze(
                                2).broadcast_to([P, 2, 2 * P]),
                            op=ALU.is_equal).then_inc(s.same, 1)

    def weigh(g, q):
        hold(dve, s.blocks, g * 2 + (q + 1), s.ticks_dve)
        v.tensor_tensor(m.weighted[:, q % 2, :, :, :],
                        m.attr[:, bass.ds(g * U + 2 * q, 2), :].unsqueeze(2).broadcast_to([P, 2, B, EDGE_DIM]),
                        m.node_hi[:, q % 2, :, 0, :].unsqueeze(3).broadcast_to([P, 2, B, EDGE_DIM]),
                        op=ALU.mult).then_inc(s.hist_in, 1)

    def begin(g, q):
        cells(g, q)
        compare(g, q)
        if not wide:
            weigh(g, q)

    def index(g, q):
        pair = slice(2 * q, 2 * q + 2)
        hold(dve, s.valued, g * U + (t0 + 2 * q + 4), s.ticks_dve)
        chain.link(v.tensor_tensor(m.late[:, :, :, :], values[:, pair, :, P:ROW], m.limit[:, :, :, :],
                                   op=ALU.is_gt))
        chain.link(v.tensor_tensor(m.spare_late[:, :, :, :], m.late[:, :, :, :],
                                   m.spare[:, :, :].rearrange("p t (w c) -> p t w c", w=2), op=ALU.mult))
        chain.link(v.tensor_tensor(m.late_row[:, :, :], m.spare_late[:, :, :, 0], m.spare_late[:, :, :, 1],
                                   op=ALU.max))
        chain.link(v.tensor_tensor(m.index[:, 4 * q:4 * q + 4].rearrange("p (j w) -> p j w", w=2),
                                   m.late_row[:, :, :], m.key[:, bass.ds(g * U + 2 * q, 2), :], op=ALU.max))
        dve.sem_inc(s.indexed, 1)

    begin(0, 0)
    with dve.Fori(0, G - 1) as g:
        chain.enter(g, 8)
        begin(g, 1)
        index(g, 0)
        begin(g, 2)
        index(g, 1)
    chain.leave(G - 1)
    begin(G - 1, 1)
    index(G - 1, 0)
    index(G - 1, 1)


def finish_blocks(nc, dve, chain, m, s, wide):
    passes, last = plan(wide)

    def finish(done, i, p):
        step, b0, n, posts = done
        normed = NORMED_BEFORE.get(step["post"], 0)
        hold(dve, s.product_ready, i * n + (posts + p + 2), s.ticks_dve)
        finish_block(nc, dve, chain, m, s, step, i * n + (b0 + p), i * n + (b0 + p + normed))

    def cast_block(g, i, j):
        if not wide:
            cast(dve, m, s, passes, g, i, j, True, s.ticks_dve)

    for g, ps in enumerate(passes):
        done = ps["done"]
        n = done[2] if done else 0

        def beside(i, j):
            if done and j in finish_at(n):
                finish(done, i, finish_at(n).index(j))

        if not (wide and done is None):
            rounds(dve, passes, g, cast_block, beside, chain, post_links(done[0]) * n if done else 0)
        dve.wait_ge(s.used, K + ps["used"] + B)
        for c, (bank, at, size) in enumerate(ps["pieces"]):
            if c % 2:
                nc.vector.tensor_copy(m.sums_t[:, at:at + size], m.acc[bank][:, 0:size]).then_inc(s.evac_dve, 1)
    with dve.Fori(0, K) as i:
        chain.enter(i, post_links(last[0]) * last[2])
        for p in range(last[2]):
            finish(last, i, p)
    chain.leave(K)


def finish_block(nc, dve, chain, m, s, step, b, normed):
    v = nc.vector
    post = step["post"]
    x = one(m.x, b)
    part = [m.product[:, D * n:D * (n + 1)] for n in range(3)]

    def by(name):
        return m.scale[name][:, bass.ds(b, 1)]

    def read():
        dve.sem_inc(s.product_read, 1)

    if post == "add_scaled":
        chain.link(v.scalar_tensor_tensor(x, part[0], by("half_inv_dst"), x, op0=ALU.mult, op1=ALU.add))
        read()
    elif post in ("layer0_end", "layer1_end", "layer2_end"):
        own, following = {"layer0_end": ("half_inv_src", "dis_dst"), "layer1_end": ("dis_dst", "dis_src"),
                          "layer2_end": ("dis_src", None)}[post]
        chain.link(v.scalar_tensor_tensor(m.xn[:, :], part[0], by(own), x, op0=ALU.mult, op1=ALU.add))
        read()
        if post == "layer1_end":
            chain.link(v.tensor_tensor(m.xn[:, :], m.xn[:, :], m.bias1[:, 1, :], op=ALU.add))
        chain.link(v.tensor_scalar(x, m.xn[:, :], 1.0, None, op0=ALU.mult))
        normalize(nc, dve, chain, m, s, normed, by(following) if following else None)
    elif post == "gcn_hidden":
        chain.link(v.scalar_tensor_tensor(m.r[:, :], part[0], by("dis_dst"), m.bias1[:, 0, :],
                                          op0=ALU.mult, op1=ALU.add))
        read()
        chain.link(v.tensor_scalar(m.v[:, :], m.r[:, :], 0.0, by("dis_dst"), op0=ALU.max, op1=ALU.mult))
    elif post == "hop":
        chain.link(v.tensor_scalar(m.v[:, :], part[0], by("dis2_src"), None, op0=ALU.mult))
        read()
    elif post == "edge0":
        chain.link(v.tensor_scalar(m.v[:, :], part[0], by("inv_dst"), None, op0=ALU.mult))
        read()
    elif post == "edge1":
        chain.link(v.tensor_scalar(m.v[:, :], part[0], by("inv_dst"), None, op0=ALU.mult))
        chain.link(v.tensor_scalar(one(m.carry, b), part[1], 1.0, None, op0=ALU.mult))
        chain.link(v.scalar_tensor_tensor(x, part[2], by("inv_dst"), x, op0=ALU.mult, op1=ALU.add))
        read()
    elif post == "edge2":
        chain.link(v.tensor_tensor(m.r[:, :], part[0], one(m.carry, b), op=ALU.add))
        chain.link(v.scalar_tensor_tensor(x, part[1], by("inv_dst"), x, op0=ALU.mult, op1=ALU.add))
        read()
        chain.link(v.tensor_scalar(m.v[:, :], m.r[:, :], by("inv_dst"), None, op0=ALU.mult))
    elif post == "edge3":
        chain.link(v.scalar_tensor_tensor(x, part[0], by("inv_dst"), x, op0=ALU.mult, op1=ALU.add))
        read()
        dve.sem_inc(s.final, 1)
    if step["xout"] is not None:
        write_table(nc, dve, chain, m, s, step["xout"], b)


def tensor_program(nc, block, a, m, s):
    @block.tensor
    def _(pe):
        mm = nc.tensor.matmul
        pe.wait_ge(s.consts, 12)
        pe.wait_ge(s.weights_in, 25 * 16)
        with pe.Fori(0, B) as b:
            hold(pe, s.pre_v, b + 1, s.ticks_pe)
            mm(m.product[:, 0:P], m.v[:, :], m.ident[:, :], start=True, stop=True).then_inc(s.pre_t, 1)
            hold(pe, s.pre_vt, b + 1, s.ticks_pe)
            mm(m.product[:, 0:D], m.vt[:, :], m.w_self[:, :], start=True, stop=False)
            mm(m.product[:, 0:D], m.ones[0:1, :], m.bias0_sum[:, :], start=False, stop=True).then_inc(s.pre_done, 1)

        for bank in m.hist_banks:
            empty(mm, m, bank)
        pe.sem_inc(s.joined, 4)
        pe.sem_inc(s.hist, 2)
        pe.sem_inc(s.key_row, 2)
        join_edges(nc, pe, m, s, False)
        pe.wait_ge(s.most, 1)
        mm(m.product[0:1, 0:P], m.most[:, 2:3], m.ident[:, :], start=True, stop=True).then_inc(s.most_row, 1)
        pe.sem_inc(s.edge_out, 2)
        with pe.Fori(0, K) as i:
            hold(pe, s.edge_blk, i + 1, s.ticks_pe)
            hold(pe, s.edge_out, i * 2 + 2, s.ticks_pe)
            for j in range(K):
                last = mm(m.edge_row[j // 4][0:EC, (j % 4) * P:(j % 4 + 1) * P], m.edge_blocks[:, j, :], m.ident[:, :],
                          start=True, stop=True)
            last.then_inc(s.edge_t, 1)

        pe.sem_inc(s.used, K)
        pe.sem_inc(s.cast_act, K)
        pe.sem_inc(s.cast_dve, K)
        pe.sem_inc(s.product_ready, 1)
        pe.sem_inc(s.product_read, 1)
        pe.wait_ge(s.flag_ready, 1)
        wide = pe.value_load(m.flag[0:1, 0:1])
        with pe.If(wide == 1):
            join_edges(nc, pe, m, s, True)
            multiply(nc, pe, m, s, True)
        with pe.Else():
            multiply(nc, pe, m, s, False)


def empty(mm, m, bank):
    mm(bank[:, 0:2], m.nought[:, :], m.nought[:, 0:2], start=True, stop=True, skip_group_check=True)


def join_edges(nc, pe, m, s, wide):
    mm = nc.tensor.matmul
    t0 = T if wide else 0

    def spread(g, q):
        for tile in range(2):
            hold(pe, s.diag, g * U + (t0 + 2 * q + tile + 1), s.ticks_pe)
            mm(m.key_row[q % 2][:, :, tile * P:(tile + 1) * P], m.ones[:, :], m.diag[:, tile, :, :],
               start=True, stop=True).then_inc(s.key_row, 1)

    def join(g, q):
        hold(pe, s.cell, g * 2 + (t0 // 2 + q + 1), s.ticks_pe)
        hold(pe, s.same, g * U + (t0 + 2 * q + 2), s.ticks_pe)
        for tile in range(2):
            hold(pe, s.valued, g * U + (t0 + 2 * q + tile + 1), s.ticks_pe)
            for w in range(2):
                for of in range(2):
                    last = mm(m.joined[tile][:, w, :], m.same[:, q, of, w, tile * P:(tile + 1) * P],
                              m.cell[:, q, of, w, :], start=(of == 0), stop=(of == 1))
            last.then_inc(s.joined, 1)

    def add_up(g, q):
        hold(pe, s.lo, g * 2 + (q + 1), s.ticks_pe)
        hold(pe, s.hist_in, g * 2 + (q + 1), s.ticks_pe)
        half = (B - B // 2) * EDGE_DIM
        for tile in range(2):
            for w in range(2):
                mm(m.edges_of[w], m.cell[:, q, tile, w, 0:P], m.node_hi[:, q, tile, w, :], start=False,
                   stop=True, skip_group_check=True)
            flat = m.weighted[:, q, tile, :, :].rearrange("p b c -> p (b c)")
            mm(m.hist_dst[0], m.node_lo[:, q, tile, :], flat[:, 0:half], start=False, stop=True,
               skip_group_check=True)
            last = mm(m.hist_dst[1], m.node_lo[:, q, tile, :], flat[:, half:B * EDGE_DIM], start=False,
                      stop=True, skip_group_check=True)
        last.then_inc(s.hist, 1)

    def pair(g, q, ahead):
        join(g, q)
        if ahead:
            spread(g, q + 2)
        if not wide:
            add_up(g, q)

    spread(0, 0)
    spread(0, 1)
    with pe.Fori(0, G - 1) as g:
        for q in range(2):
            pair(g, q, True)
    pair(G - 1, 0, False)
    pair(G - 1, 1, False)


def multiply(nc, pe, m, s, wide):
    mm = nc.tensor.matmul
    passes, last = plan(wide)
    evacuated = [0, 0]
    taken = {}

    def product(done, i, p):
        step, _, n, posts = done
        index = i * n + (posts + p)
        wide_w = len(step["w"]) * D
        if step["w"] == ("ident",):
            w = m.ident[:, :]
        else:
            first = m.w_at[step["w"][0]]
            w = m.w[:, first:first + len(step["w"]), :].rearrange("p n d -> p (n d)")
        hold(pe, s.slot_ready, index + 1, s.ticks_pe)
        edge = step.get("edge")
        done_ = mm(m.product[:, 0:wide_w], m.sums_slot[:, :], w, start=True, stop=edge is None)
        if edge:
            fed = posts - EDGE_POSTS_BEFORE
            hold(pe, s.edge_ready, i * (16 * n) + 16 * (fed + p + 1), s.ticks_pe)
            done_ = mm(m.product[:, 0:D], m.edge_slot[:, :], m.w_edge[:, int(edge[1]), :], start=False, stop=True)
        done_.then_inc(s.product_ready, 1)

    for g, ps in enumerate(passes):
        step, done, pieces = ps["step"], ps["done"], ps["pieces"]
        for bank, _, size in pieces:
            if bank in taken:
                pe.wait_ge(*taken[bank])
            empty(mm, m, m.acc[bank])
        for c, (bank, _, _) in enumerate(pieces):
            evacuated[c % 2] += 1
            taken[bank] = (s.evac_dve if c % 2 else s.evac_act, evacuated[c % 2])

        def one_round(i, own):
            for j in range(K):
                if wide:
                    hold(pe, s.rows_in[j], rows_count(g, i, j), s.ticks_pe)
                rows = m.ring_wide if wide else m.rows_r
                hold(pe, s.staged, i * K + (ps["used"] + j + 1), s.ticks_pe)
                if wide:
                    parts = [m.staged_wide[:, j % RING, :]]
                else:
                    parts = [m.staged_r[:, j % RING, half, :] for half in range(2)]
                for part in parts:
                    for bank, at, size in pieces:
                        last_mm = mm(m.acc[bank][:, 0:size], part, rows[:, j % RING, at:at + size],
                                     start=False, stop=True, skip_group_check=True)
                        if own is not None and at <= own + j * P < at + size:
                            last_mm = mm(m.acc[bank][:, own + j * P - at:own + (j + 1) * P - at], part,
                                         m.ident[:, :] if wide else m.ident_r[:, :], start=False, stop=True,
                                         skip_group_check=True)
                last_mm.then_inc(s.used, 1)
                if done and j in product_at(done[2]):
                    product(done, i, product_at(done[2]).index(j))

        first = ps["b0"] // K if step["loop"] else 0
        end = first + ps["n"] if step["loop"] else 0
        if first > 0:
            with pe.Fori(0, first) as i:
                one_round(i, None)
        for i in range(first, end):
            one_round(i, (i - first) * K * P)
        if end < K:
            with pe.Fori(end, K) as i:
                one_round(i, None)
    with pe.Fori(0, K) as i:
        for p in range(last[2]):
            product(last, i, p)


EDGE_POSTS_BEFORE = B * next(n for n, step in enumerate(STEPS) if "edge" in step)


_INS = ["x", "src", "dst", "edge_attr_16", "L0_gnn_W_self", "L0_gnn_b_self", "L0_gnn_W_s2d", "L0_gnn_b_s2d",
        "L0_gnn_W_d2s", "L0_gnn_b_d2s", "L1_gnn_W1", "L1_gnn_b1", "L1_gnn_W2", "L1_gnn_b2", "L3_gnn_W0",
        "L3_gnn_b0", "L3_gnn_W1", "L3_gnn_b1", "L3_gnn_W2", "L3_gnn_b2", "L3_gnn_W3", "L3_gnn_b3"]


def arguments(t):
    w1, w2, w3 = t["L3_gnn_W1"], t["L3_gnn_W2"], t["L3_gnn_W3"]
    a = Names()
    a.x, a.src, a.dst, a.edge_attr, a.out = t["x"], t["src"], t["dst"], t["edge_attr_16"], t["out"]
    a.w_self = t["L0_gnn_W_self"]
    a.w = dict(s2d=t["L0_gnn_W_s2d"], d2s=t["L0_gnn_W_d2s"], g1=t["L1_gnn_W1"], g2=t["L1_gnn_W2"],
               e0=t["L3_gnn_W0"][0:D, :], e1=w1[0:D, :], e2a=w2[0:D, :], e2b=w2[D:2 * D, :],
               e3a=w3[0:D, :], e3b=w3[D:2 * D, :], e3c=w3[2 * D:3 * D, :])
    a.w_edge = [t["L3_gnn_W0"][D:D + EDGE_DIM, :], w1[D:D + EDGE_DIM, :], w2[2 * D:2 * D + EDGE_DIM, :],
                w3[3 * D:3 * D + EDGE_DIM, :]]
    a.b_edge = [t[f"L3_gnn_b{n}"] for n in range(4)]
    a.bias0 = [t["L0_gnn_b_self"], t["L0_gnn_b_s2d"], t["L0_gnn_b_d2s"]]
    a.bias1 = [t["L1_gnn_b1"], t["L1_gnn_b2"]]
    return a


def kernel(**inputs):
    import concourse.bacc as _bacc
    from concourse.bass_utils import run_bass_kernel_spmd as _run

    nc = _bacc.Bacc("TRN2", target_bir_lowering=False, num_devices=1)
    arrays, t = {}, {}
    for name in _INS:
        array = np.ascontiguousarray(inputs[name])
        arrays[f"in_{name}_dram"] = array
        t[name] = nc.dram_tensor(f"in_{name}_dram", array.shape, mybir.dt.from_np(array.dtype),
                                 kind="ExternalInput").ap()
    t["out"] = nc.dram_tensor("out_0_dram", (N, D), F32, kind="ExternalOutput").ap()
    build_gnn(nc, arguments(t))
    r = _run(nc, [arrays], core_ids=[0])
    return r.results[0]["out_0_dram"]
```
